# Optimizing a Trainium2 kernel written in Bass

```python
import numpy as np
import jax
import jax.numpy as jnp

def _softmax(x, axis=-1):
    return jax.nn.softmax(x, axis=axis)

def _gelu(x):
    return jax.nn.gelu(x, approximate=True)

def _silu(x):
    return jax.nn.silu(x)

def _sigmoid(x):
    return jax.nn.sigmoid(x)

def _layernorm(x, axis=-1, eps=1e-05):
    m = jnp.mean(x, axis=axis, keepdims=True)
    v = jnp.var(x, axis=axis, keepdims=True)
    return (x - m) / jnp.sqrt(v + eps)

def _scatter_add(tgt, idx, src, axis=0):
    return tgt.at[idx].add(src)

def _segment_sum(src, seg, n):
    return jax.ops.segment_sum(src, seg, n)
kernel_name = 'mk_perceiver_d1_seqx_r8_f64f98'

def setup_inputs(seed: int=0):
    np.random.seed(seed)
    _w = jnp.asarray

    def _rec_inputs():
        import jax
        import jax.numpy as jnp
        _rk = jax.random.key(seed)
        x = -0.0003929 + 0.9999 * jax.random.normal(jax.random.fold_in(_rk, 1), (1, 64, 256), jnp.float32)
        _lenS = 64 - jax.random.randint(jax.random.fold_in(_rk, 7), (1,), 0, max(1, 64 // 4) + 1, jnp.int32)
        _lenS2 = 6272 - jax.random.randint(jax.random.fold_in(_rk, 8), (1,), 0, max(1, 6272 // 4) + 1, jnp.int32)
        _ctx_2048P = jax.random.normal(jax.random.fold_in(_rk, 11), (1, 16, 256), jnp.float32)
        _ctx_2048c = jax.random.dirichlet(jax.random.fold_in(_rk, 511), 0.3 * jnp.ones((16,), jnp.float32), (1, 6272))
        _ctx_2048t = jnp.einsum('bsk,bkd->bsd', _ctx_2048c, _ctx_2048P)
        _ctx_2048t = _ctx_2048t * jax.lax.rsqrt(jnp.mean(jnp.square(_ctx_2048t)) + 1e-12) * 0.953939
        ctx_2048 = -1.39393e-06 + 0.999914 * (_ctx_2048t + 0.3 * jax.random.normal(jax.random.fold_in(_rk, 611), (1, 6272, 256), jnp.float32))
        itok_BxS_0_1023 = jax.random.randint(jax.random.fold_in(_rk, 12), (1, 64), 0, 128, jnp.int32)
        return (x, ctx_2048, itok_BxS_0_1023)
    x, ctx_2048, itok_BxS_0_1023 = _rec_inputs()

    def _L0_xattn_setup():
        import jax, jax.numpy as jnp
        import numpy as np
        B, Lq, Lk = (2, 512, 128)
        Q_DIM, KV_DIM = (256, 256)
        H, HD = (16, 128)
        KVC, QC, R = (64, 96, 64)
        LOOKBACK = 8
        NEG = -1e+30

        def _rope(x, L):
            half = x.shape[-1] // 2
            inv_freq = 1.0 / 10000.0 ** (jnp.arange(half, dtype=jnp.float32) / half)
            ang = jnp.arange(L, dtype=jnp.float32)[:, None] * inv_freq
            cos, sin = (jnp.cos(ang), jnp.sin(ang))
            x1, x2 = (x[..., :half], x[..., half:])
            return jnp.concatenate([x1 * cos - x2 * sin, x1 * sin + x2 * cos], axis=-1)
        key = jax.random.key(seed)
        ks = jax.random.split(key, 11)

        def w(k, shape, fan_in):
            return jax.random.normal(k, shape, jnp.float32) / np.sqrt(fan_in).astype(np.float32)
        return {'q': jax.random.normal(ks[0], (B, Lq, Q_DIM), jnp.float32), 'kv': jax.random.normal(ks[1], (B, Lk, KV_DIM), jnp.float32), 'seg_id': jnp.sort(jax.random.randint(ks[2], (B, Lq), 0, Lk), axis=-1), 'W_kvc': w(ks[3], (KV_DIM, KVC), KV_DIM), 'W_dq': w(ks[4], (Q_DIM, QC), Q_DIM), 'W_uq': w(ks[5], (QC, H * HD), QC), 'W_qr': w(ks[6], (QC, H * R), QC), 'W_uk': w(ks[7], (KVC, H * HD), KVC), 'W_kr': w(ks[8], (KVC, R), KVC), 'W_uv': w(ks[9], (KVC, H * HD), KVC), 'W_o': w(ks[10], (H * HD, Q_DIM), H * HD)}
    _L0_xattn_all = _L0_xattn_setup()
    _L0_xattn_in = {k: v for k, v in _L0_xattn_all.items() if k in ('W_kvc', 'W_dq', 'W_uq', 'W_qr', 'W_uk', 'W_kr', 'W_uv', 'W_o')}
    del _L0_xattn_all

    def _L0_attn_setup():
        import jax, jax.numpy as jnp
        import numpy as np
        H = 16
        NORM = 16.0
        SCALE = 128.0 ** (-0.5)
        EPS = 1e-05

        def _gla_core(x, Wq, Wk, Wkg1, Wkg2, bkg2, Wv, Wg, bg, Wo):
            B, L, D = x.shape
            q = x @ Wq.T
            k = x @ Wk.T * SCALE
            kg = x @ Wkg1.T @ Wkg2.T + bkg2
            v = x @ Wv.T
            gproj = x @ Wg.T + bg
            dk = q.shape[-1] // H
            dv = D // H
            heads = lambda t, dh: t.reshape(B, L, H, dh).transpose(0, 2, 1, 3)
            qh = heads(q, dk)
            kh = heads(k, dk)
            vh = heads(v, dv)
            gk = jax.nn.log_sigmoid(heads(kg, dk)) / NORM
            tfirst = lambda t: t.transpose(2, 0, 1, 3)

            def step(S, inp):
                qt, kt, vt, gt = inp
                S = S * jnp.exp(gt)[..., None] + kt[..., None] * vt[..., None, :]
                ot = jnp.einsum('bhk,bhkv->bhv', qt, S)
                return (S, ot)
            S0 = jnp.zeros((B, H, dk, dv), x.dtype)
            _, os = jax.lax.scan(step, S0, (tfirst(qh), tfirst(kh), tfirst(vh), tfirst(gk)))
            o = os.transpose(1, 2, 0, 3)
            mu = o.mean(-1, keepdims=True)
            var = ((o - mu) ** 2).mean(-1, keepdims=True)
            o = (o - mu) * jax.lax.rsqrt(var + EPS)
            o = o.transpose(0, 2, 1, 3).reshape(B, L, D)
            return jax.nn.silu(gproj) * o @ Wo.T
        key = jax.random.key(seed)
        ks = jax.random.split(key, 10)
        B, L, D = (2, 256, 256)
        g = lambda k, shape, s: jax.random.normal(k, shape, jnp.float32) * s
        return {'x': g(ks[0], (B, L, D), 1.0), 'Wq': g(ks[1], (128, D), 0.02), 'Wk': g(ks[2], (128, D), 0.02), 'Wkg1': g(ks[3], (16, D), 0.02), 'Wkg2': g(ks[4], (128, 16), 0.05), 'bkg2': jnp.zeros((128,), jnp.float32), 'Wv': g(ks[5], (D, D), 0.02), 'Wg': g(ks[6], (D, D), 0.02), 'bg': jnp.zeros((D,), jnp.float32), 'Wo': g(ks[7], (D, D), 0.02)}
    _L0_attn_all = _L0_attn_setup()
    _L0_attn_in = {k: v for k, v in _L0_attn_all.items() if k in ('Wq', 'Wk', 'Wkg1', 'Wkg2', 'bkg2', 'Wv', 'Wg', 'bg', 'Wo')}
    del _L0_attn_all

    def _L0_ffn_setup():
        import jax, jax.numpy as jnp
        import numpy as np
        TOP_K = 2
        EPS = 1e-06
        key = jax.random.key(seed)
        ks = jax.random.split(key, 5)
        B, S, D, E = (4, 256, 256, 8)
        sd = 1.0 / np.sqrt(D)
        return {'x': jax.random.normal(ks[0], (B, S, D), jnp.float32), 'router_w': jax.random.normal(ks[1], (D, E), jnp.float32) * sd, 'router_b': jnp.zeros((E,), jnp.float32), 'expert_w': jax.random.normal(ks[2], (E, D, D), jnp.float32) * sd, 'expert_b': jnp.zeros((E, D), jnp.float32), 'proj_w': jax.random.normal(ks[3], (D, D), jnp.float32) * sd, 'proj_b': jnp.zeros((D,), jnp.float32), 'norm_w': jnp.ones((D,), jnp.float32)}
    _L0_ffn_all = _L0_ffn_setup()
    _L0_ffn_in = {k: v for k, v in _L0_ffn_all.items() if k in ('router_w', 'router_b', 'expert_w', 'expert_b', 'proj_w', 'proj_b', 'norm_w')}
    del _L0_ffn_all
    return {'x': x, 'ctx_2048': ctx_2048, 'itok_BxS_0_1023': itok_BxS_0_1023, 'L0_xattn_W_kvc': _L0_xattn_in['W_kvc'], 'L0_xattn_W_dq': _L0_xattn_in['W_dq'], 'L0_xattn_W_uq': _L0_xattn_in['W_uq'], 'L0_xattn_W_qr': _L0_xattn_in['W_qr'], 'L0_xattn_W_uk': _L0_xattn_in['W_uk'], 'L0_xattn_W_kr': _L0_xattn_in['W_kr'], 'L0_xattn_W_uv': _L0_xattn_in['W_uv'], 'L0_xattn_W_o': _L0_xattn_in['W_o'], 'L0_attn_Wq': _L0_attn_in['Wq'], 'L0_attn_Wk': _L0_attn_in['Wk'], 'L0_attn_Wkg1': _L0_attn_in['Wkg1'], 'L0_attn_Wkg2': _L0_attn_in['Wkg2'], 'L0_attn_bkg2': _L0_attn_in['bkg2'], 'L0_attn_Wv': _L0_attn_in['Wv'], 'L0_attn_Wg': _L0_attn_in['Wg'], 'L0_attn_bg': _L0_attn_in['bg'], 'L0_attn_Wo': _L0_attn_in['Wo'], 'L0_ffn_router_w': _L0_ffn_in['router_w'], 'L0_ffn_router_b': _L0_ffn_in['router_b'], 'L0_ffn_expert_w': _L0_ffn_in['expert_w'], 'L0_ffn_expert_b': _L0_ffn_in['expert_b'], 'L0_ffn_proj_w': _L0_ffn_in['proj_w'], 'L0_ffn_proj_b': _L0_ffn_in['proj_b'], 'L0_ffn_norm_w': _L0_ffn_in['norm_w']}

def reference(x, ctx_2048, itok_BxS_0_1023, L0_xattn_W_kvc, L0_xattn_W_dq, L0_xattn_W_uq, L0_xattn_W_qr, L0_xattn_W_uk, L0_xattn_W_kr, L0_xattn_W_uv, L0_xattn_W_o, L0_attn_Wq, L0_attn_Wk, L0_attn_Wkg1, L0_attn_Wkg2, L0_attn_bkg2, L0_attn_Wv, L0_attn_Wg, L0_attn_bg, L0_attn_Wo, L0_ffn_router_w, L0_ffn_router_b, L0_ffn_expert_w, L0_ffn_expert_b, L0_ffn_proj_w, L0_ffn_proj_b, L0_ffn_norm_w):
    import jax
    import jax.numpy as jnp

    def _L0_xattn_ref(q, kv, seg_id, W_kvc, W_dq, W_uq, W_qr, W_uk, W_kr, W_uv, W_o):
        import jax, jax.numpy as jnp
        import numpy as np
        B, Lq, Lk = (2, 512, 128)
        Q_DIM, KV_DIM = (256, 256)
        H, HD = (16, 128)
        KVC, QC, R = (64, 96, 64)
        LOOKBACK = 8
        NEG = -1e+30

        def _rope(x, L):
            half = x.shape[-1] // 2
            inv_freq = 1.0 / 10000.0 ** (jnp.arange(half, dtype=jnp.float32) / half)
            ang = jnp.arange(L, dtype=jnp.float32)[:, None] * inv_freq
            cos, sin = (jnp.cos(ang), jnp.sin(ang))
            x1, x2 = (x[..., :half], x[..., half:])
            return jnp.concatenate([x1 * cos - x2 * sin, x1 * sin + x2 * cos], axis=-1)
        b, lq, _ = q.shape
        lk = kv.shape[1]
        kv_c = kv @ W_kvc
        q_c = q @ W_dq
        q_nope = (q_c @ W_uq).reshape(b, lq, H, HD).transpose(0, 2, 1, 3)
        q_rope = (q_c @ W_qr).reshape(b, lq, H, R).transpose(0, 2, 1, 3)
        k_nope = (kv_c @ W_uk).reshape(b, lk, H, HD)
        v = (kv_c @ W_uv).reshape(b, lk, H, HD)
        k_rope = kv_c @ W_kr
        q_rope = _rope(q_rope, lq)
        k_rope = _rope(k_rope, lk)
        scale = 1.0 / np.sqrt(HD + R).astype(np.float32)
        scores = (jnp.einsum('bhqd,bkhd->bhqk', q_nope, k_nope) + jnp.einsum('bhqr,bkr->bhqk', q_rope, k_rope)) * scale
        k_ids = jnp.arange(lk)[None, None, :]
        qs = seg_id[:, :, None]
        good = (k_ids <= qs) & (k_ids >= qs - LOOKBACK)
        scores = jnp.where(good[:, None, :, :], scores, NEG)
        attn = jax.nn.softmax(scores, axis=-1)
        out = jnp.einsum('bhqk,bkhd->bqhd', attn, v).reshape(b, lq, H * HD)
        return out @ W_o

    def _L0_attn_ref(x, Wq, Wk, Wkg1, Wkg2, bkg2, Wv, Wg, bg, Wo):
        import jax, jax.numpy as jnp
        import numpy as np
        H = 16
        NORM = 16.0
        SCALE = 128.0 ** (-0.5)
        EPS = 1e-05

        def _gla_core(x, Wq, Wk, Wkg1, Wkg2, bkg2, Wv, Wg, bg, Wo):
            B, L, D = x.shape
            q = x @ Wq.T
            k = x @ Wk.T * SCALE
            kg = x @ Wkg1.T @ Wkg2.T + bkg2
            v = x @ Wv.T
            gproj = x @ Wg.T + bg
            dk = q.shape[-1] // H
            dv = D // H
            heads = lambda t, dh: t.reshape(B, L, H, dh).transpose(0, 2, 1, 3)
            qh = heads(q, dk)
            kh = heads(k, dk)
            vh = heads(v, dv)
            gk = jax.nn.log_sigmoid(heads(kg, dk)) / NORM
            tfirst = lambda t: t.transpose(2, 0, 1, 3)

            def step(S, inp):
                qt, kt, vt, gt = inp
                S = S * jnp.exp(gt)[..., None] + kt[..., None] * vt[..., None, :]
                ot = jnp.einsum('bhk,bhkv->bhv', qt, S)
                return (S, ot)
            S0 = jnp.zeros((B, H, dk, dv), x.dtype)
            _, os = jax.lax.scan(step, S0, (tfirst(qh), tfirst(kh), tfirst(vh), tfirst(gk)))
            o = os.transpose(1, 2, 0, 3)
            mu = o.mean(-1, keepdims=True)
            var = ((o - mu) ** 2).mean(-1, keepdims=True)
            o = (o - mu) * jax.lax.rsqrt(var + EPS)
            o = o.transpose(0, 2, 1, 3).reshape(B, L, D)
            return jax.nn.silu(gproj) * o @ Wo.T
        return _gla_core(x, Wq, Wk, Wkg1, Wkg2, bkg2, Wv, Wg, bg, Wo)

    def _L0_ffn_ref(x, router_w, router_b, expert_w, expert_b, proj_w, proj_b, norm_w):
        import jax, jax.numpy as jnp
        import numpy as np
        TOP_K = 2
        EPS = 1e-06
        B, S, D = x.shape
        E = router_b.shape[0]
        logits = jnp.einsum('bsd,de->bse', x, router_w) + router_b
        topk_vals, topk_idx = jax.lax.top_k(logits, TOP_K)
        topk_w = jax.nn.softmax(topk_vals, axis=-1)
        full_w = jnp.sum(jax.nn.one_hot(topk_idx, E, dtype=x.dtype) * topk_w[..., None], axis=-2)
        xf = x.reshape(-1, D)
        h = jnp.einsum('td,edf->etf', xf, expert_w) + expert_b[:, None, :]
        expert_out = jax.nn.silu(h)
        combined = jnp.einsum('etf,te->tf', expert_out, full_w.reshape(-1, E)).reshape(B, S, D)
        out = jnp.einsum('bsd,df->bsf', combined, proj_w) + proj_b
        y = x + out
        rms = jnp.sqrt(jnp.mean(y * y, axis=-1, keepdims=True) + EPS)
        return norm_w * (y / rms)
    x = x + _L0_xattn_ref(_layernorm(x, axis=-1), ctx_2048, itok_BxS_0_1023, L0_xattn_W_kvc, L0_xattn_W_dq, L0_xattn_W_uq, L0_xattn_W_qr, L0_xattn_W_uk, L0_xattn_W_kr, L0_xattn_W_uv, L0_xattn_W_o)
    x = x + _L0_attn_ref(_layernorm(x, axis=-1), L0_attn_Wq, L0_attn_Wk, L0_attn_Wkg1, L0_attn_Wkg2, L0_attn_bkg2, L0_attn_Wv, L0_attn_Wg, L0_attn_bg, L0_attn_Wo)
    x = x + _L0_ffn_ref(_layernorm(x, axis=-1), L0_ffn_router_w, L0_ffn_router_b, L0_ffn_expert_w, L0_ffn_expert_b, L0_ffn_proj_w, L0_ffn_proj_b, L0_ffn_norm_w)
    return x

_drawn_inputs = setup_inputs


def setup_inputs(seed=0):
    import zlib

    import numpy as np

    out = dict(_drawn_inputs(seed))
    spreads = {'L0_attn_bkg2': (0.0, 2.0),
     'L0_attn_bg': (0.0, 0.577),
     'L0_ffn_router_b': (0.0, 0.692),
     'L0_ffn_expert_b': (0.0, 0.403),
     'L0_ffn_proj_b': (0.0, 0.1),
     'L0_ffn_norm_w': (1.0, 0.2)}
    factors = {'L0_attn_Wkg1': 8.0, 'L0_attn_Wkg2': 8.0}
    for name, (base, spread) in spreads.items():
        noise = np.random.default_rng([zlib.crc32(name.encode()), seed]).standard_normal(out[name].shape)
        drawn = base * np.exp(spread * noise) if base else spread * noise
        out[name] = jnp.asarray(drawn.astype(out[name].dtype))
    for name, factor in factors.items():
        out[name] = (out[name] * factor).astype(out[name].dtype)
    return out
```

```python
from contextlib import ExitStack

import numpy as np

import concourse.bass as bass
from concourse import mybir

F32 = mybir.dt.float32
I32 = mybir.dt.int32
U32 = mybir.dt.uint32
ALU = mybir.AluOpType
ACT = mybir.ActivationFunctionType
AX = mybir.AxisListType
RADD = bass.bass_isa.ReduceOp.add

P = 128
T = 64
D = 256
DC = D // P
LK = 6272
H = 16
HP = H // 2
HD = 128
KVC, QC, R = 64, 96, 64
HALF = R // 2
LOOKBACK = 8
WIN = LOOKBACK + 1
NKEY = T * WIN
NG = -(-NKEY // P)
MROW = 7
MTURN = LK // P // MROW
ROW = D + R
QPC = 8
NCH = T // QPC
KPC = QPC * WIN
NEG = -1e30
SHIFT = 1000.0
QK_SCALE = float(1.0 / np.sqrt(np.float32(HD + R)))
LN_EPS = 1e-5
DK, DV = 8, 16
GLR = 16
GK_SCALE = 128.0 ** -0.5
GATE_NORM = 16.0
GLA_EPS = 1e-5
E = 8
EH = E // 2
RMS_EPS = 1e-6

C1 = dict(ident=P, dq=DC * QC, koff=NG, moff=WIN)
C2 = dict(kw=DC * 2 * KVC, kvct=D, kr=R, block=KPC, cosq=NG * HALF, sinq=NG * HALF,
          headsum=H, twice=T, iota=E)
GLA = dict(q=P, k=P, kg1=GLR, v=D, g=D, o=D)
ROWS = dict(bg=D, proj_b=D, norm_w=D, router_b=E)


def width(parts):
    return sum(parts.values())


def place(parts, name):
    at = 0
    for n, w in parts.items():
        if n == name:
            return at, at + w
        at += w
    raise KeyError(name)


def block_kernel(nc, seg_in, x_in, c1_in, c2_in, ctx_in, uqk_in, qr_in, uv_in, wo_in, gla_in,
                 kg2_in, rows_in, router_in, expert_in, expert_b_in, proj_in, out):
    with ExitStack() as ctx:
        def sb(name, cols, dt=F32, rows=P):
            return ctx.enter_context(nc.sbuf_tensor(name, [rows, *cols], dt))

        def sem(name):
            return ctx.enter_context(nc.semaphore(name))

        bank = [ctx.enter_context(nc.psum_tensor(f"bank{i}", [P, 512], F32)) for i in range(8)]

        seg = sb("seg", [NG + T], I32)
        x = sb("x", [D])
        c1 = sb("c1", [width(C1)])
        c2 = sb("c2", [width(C2)])
        keys = sb("keys", [NG, ROW])
        uqk = sb("uqk", [H, QC + KVC])
        aq = sb("aq", [H, 2, KVC])
        uv = sb("uv", [H, KVC])
        wo = sb("wo", [H, D])
        gla = sb("gla", [DC, width(GLA)])
        kg2 = sb("kg2", [P + 1])
        rows = sb("rows", [width(ROWS)])
        router = sb("router", [DC, E])
        expert = sb("expert", [DC, E, D])
        expert_b = sb("expert_b", [EH * D])
        proj = sb("proj", [DC, D])

        def value_columns(j):
            v = bank[2 + j][0:T, 0:P].rearrange("t (h v) -> t v h", v=8)
            return v.unsqueeze(3).broadcast_to([T, 8, H, DK])

        def c1_(name):
            a, b = place(C1, name)
            return c1[:, a:b]

        def c2_(name):
            a, b = place(C2, name)
            return c2[:, a:b]

        def gla_(kc, name):
            a, b = place(GLA, name)
            return gla[:, kc, a:b]

        def rows_(name, n=T):
            a, b = place(ROWS, name)
            return rows[0:n, a:b]

        ident = c1_("ident")
        kw = c2_("kw").rearrange("p (c n) -> p c n", c=DC)
        kw_kr = c2_("kw").rearrange("p (c s n) -> p c s n", c=DC, s=2)[:, :, 1, :]
        dq = c1_("dq").rearrange("p (c n) -> p c n", c=DC)
        cosq = c2_("cosq").rearrange("p (g r) -> p g r", g=NG)
        sinq = c2_("sinq").rearrange("p (g r) -> p g r", g=NG)

        segf = sb("segf", [NG + T])
        segc = sb("segc", [NG + T])
        inside = sb("inside", [NG + T])
        outside = sb("outside", [NG])
        lowest = sb("lowest", [1])
        flag = sb("flag", [1], I32)
        kidx = sb("kidx", [NG])
        kidxu = sb("kidxu", [NG], U32)
        segv = sb("segv", [T])
        pos = sb("pos", [T, WIN])
        posc = sb("posc", [T, WIN])
        maskb = sb("maskb", [NCH, KPC])
        wide = sb("wide", [MROW, D])
        sums = sb("sums", [MROW, D])
        total = sb("total", [D])
        share = sb("share", [D])
        consts = sb("consts", [3])
        eps5, eps6, one = consts[:, 0:1], consts[:, 1:2], consts[:, 2:3]
        stats = sb("stats", [4, 6])
        mv = sb("mv", [4, 2])
        lnv = sb("lnv", [4])
        rstd = sb("rstd", [4])
        xn1 = sb("xn1", [D])
        xn1t = sb("xn1t", [DC * T])
        qct = sb("qct", [T])
        qt = sb("qt", [NCH, H, QPC])
        kt_in = sb("kt_in", [DC, NG * P])
        kv = sb("kv", [NG, 2, KVC])
        kr_ = sb("kr_", [NG, 2 * KVC])
        cosr = sb("cosr", [NG, HALF])
        sinr = sb("sinr", [NG, HALF])
        rt = sb("rt", [4, NG, HALF])
        ru = sb("ru", [NG, 2, HALF])
        rw = sb("rw", [NG, 2, HALF])
        kt = sb("kt", [NG * P])
        vals = sb("vals", [NCH, KVC])
        s = sb("s", [NCH, KPC])
        nmax = sb("nmax", [NCH])
        p = sb("p", [NCH, KPC])
        psums = sb("psums", [NCH])
        rsum = sb("rsum", [NCH])
        pt = sb("pt", [NCH, P])
        ctxt = sb("ctxt", [HP, T])
        wvo = sb("wvo", [HP, D])
        x1 = sb("x1", [D])

        xn2 = sb("xn2", [D])
        xn2t = sb("xn2t", [DC * T])
        kg1 = sb("kg1", [T])
        z = sb("z", [T])
        nabs = sb("nabs", [T])
        minz = sb("minz", [T])
        ez = sb("ez", [T])
        lz = sb("lz", [T])
        logsig = sb("logsig", [T])
        gate = sb("gate", [T])
        gates = sb("gates", [DV, T])
        qs = sb("qs", [T])
        ks = sb("ks", [T])
        vrep = sb("vrep", [DV, H, DK])
        kvt = sb("kvt", [DV, T])
        state = sb("state", [DV, T])
        qstate = sb("qstate", [DV, T])
        zg = sb("zg", [D])
        eg = sb("eg", [D])
        eg1 = sb("eg1", [D])
        rg = sb("rg", [D])
        sg = sb("sg", [D])
        osum = sb("osum", [H])
        oc = sb("oc", [H, DV])
        osq = sb("osq", [H, DV])
        ovar = sb("ovar", [H])
        olnv = sb("olnv", [H])
        orstd = sb("orstd", [H])
        ocs = sb("ocs", [H, DV])
        og = sb("og", [H, DV])
        ogt = sb("ogt", [DC * T])
        x2 = sb("x2", [D])

        xn3 = sb("xn3", [D])
        xn3t = sb("xn3t", [DC * T])
        xb = sb("xb", [D])
        logits = sb("logits", [E])
        top = sb("top", [8])
        topi = sb("topi", [8], U32)
        topf = sb("topf", [8])
        gap = sb("gap", [1])
        egap = sb("egap", [1])
        egap1 = sb("egap1", [1])
        w1 = sb("w1", [1])
        w2 = sb("w2", [1])
        fw1 = sb("fw1", [E])
        fw2 = sb("fw2", [E])
        fw = sb("fw", [EH])
        h = state[:].rearrange("p (j v) t -> p j (v t)", j=2)
        hs = kvt[:].rearrange("p (j v) t -> p j (v t)", j=2)
        comb = qstate[:].rearrange("p (e v) t -> p e (v t)", e=EH)
        combt = sb("combt", [DC * T])
        y = sb("y", [D])
        ysq = sb("ysq", [D])
        yss = sb("yss", [1])
        ylnv = sb("ylnv", [1])
        yr = sb("yr", [1])
        yn = sb("yn", [D])
        fin = sb("fin", [D])

        landed = {n: sem(f"landed_{n}") for n in (
            "seg", "x", "c1", "c2", "uqk", "qr", "uv", "gla", "kg2", "rows", "router",
            "expert_b", "proj", "out", "wide")}
        landed_key = [sem(f"landed_key{g}") for g in range(NG)]
        landed_wo = [sem(f"landed_wo{i}") for i in range(2)]
        landed_expert = [sem(f"landed_expert{i}") for i in range(2)]
        done = {n: sem(f"done_{n}") for n in (
            "consts", "sums", "kidx", "flag", "keys", "cosr", "maskb",
            "mv1", "rstd1", "xn1", "xn1t_ps", "xn1t", "wkk_ps", "wkk", "qct_ps", "qct",
            "aq_ps", "aq", "kin_ps", "kin", "qt_ps", "qt", "kv_ps", "kv", "kr", "kt_ps", "kt",
            "vals_ps", "vals", "s_ps", "s", "nmax", "exp", "p", "pt_ps", "pt", "wvo_ps", "wvo",
            "ctx_ps", "ctx", "y1_ps", "x1",
            "mv2", "rstd2", "xn2", "xn2t_ps", "xn2t", "kg1_ps", "kg1", "v_ps", "v", "qk_ps",
            "qs", "ks", "kg_ps", "nabs", "lz", "logsig", "gate", "gates", "g_ps", "zg", "eg",
            "eg1", "rg", "sg", "vrep_ps", "kvt", "qstate", "o_ps", "oc", "osq", "ovar", "orstd",
            "og", "ogt_ps", "ogt", "y2_ps", "x2",
            "mv3", "rstd3", "xn3", "xn3t_ps", "xn3t", "lg_ps", "gap", "egap", "h_ps", "h",
            "hs", "comb", "combt_ps", "combt", "y3_ps", "y", "yss", "yr", "fin")}
        pool_step = sem("pool_step")
        mean_step = sem("mean_step")
        act_step = sem("act_step")
        dve_step = sem("dve_step")

        def stepper(eng, step_sem):
            count = [0]

            def after(ins):
                count[0] += 1
                ins.then_inc(step_sem, 1)
                eng.wait_ge(step_sem, count[0])
            return after

        block = ctx.enter_context(nc.Block())

        @block.sync
        def _(sp):
            def load(dst, src, signal):
                sp.dma_start(dst, src).then_inc(signal, 16)

            load(seg[:], seg_in, landed["seg"])
            load(c1[:], c1_in, landed["c1"])
            load(c2[:], c2_in, landed["c2"])
            load(uqk[:].rearrange("p h n -> p (h n)"), uqk_in, landed["uqk"])
            load(aq[0:QC, :, 1, :], qr_in.rearrange("q (h r) -> q h r", h=H), landed["qr"])
            load(uv[:].rearrange("p h n -> p (h n)"), uv_in, landed["uv"])
            for i in range(2):
                load(wo[:, i * HP:(i + 1) * HP, :].rearrange("p h n -> p (h n)"),
                     wo_in[:, i * HP * D:(i + 1) * HP * D], landed_wo[i])
            load(gla[:].rearrange("p c n -> p (c n)"), gla_in, landed["gla"])
            load(kg2[:], kg2_in, landed["kg2"])
            load(rows[:], rows_in.broadcast_to([P, width(ROWS)]), landed["rows"])
            load(router[:].rearrange("p c n -> p (c n)"), router_in, landed["router"])
            for g in range(2):
                load(expert_b[g * T:(g + 1) * T, :],
                     expert_b_in[g:g + 1, :].broadcast_to([T, EH * D]), landed["expert_b"])
            for kc in range(DC):
                load(expert[:, kc].rearrange("p e n -> p (e n)"),
                     expert_in[:, kc * E * D:(kc + 1) * E * D], landed_expert[kc])
            load(proj[:].rearrange("p c n -> p (c n)"), proj_in, landed["proj"])
            sp.wait_ge(done["fin"], 1)
            sp.dma_start(out, fin[0:T, :]).then_inc(landed["out"], 16)
            sp.wait_ge(landed["out"], 16)

        @block.gpsimd
        def _(pool):
            after = stepper(pool, pool_step)
            pool.wait_ge(done["kidx"], 1)
            for g in range(NG):
                pool.indirect_dma_start(
                    out=keys[:, g, :], out_offset=None, in_=ctx_in,
                    in_offset=bass.IndirectOffsetOnAxis(ap=kidxu[:, g:g + 1], axis=0),
                ).then_inc(landed_key[g], 16)
            pool.wait_ge(done["flag"], 1)
            some_outside = nc.values_load(flag[0:1, 0:1], engines=[mybir.EngineType.Pool],
                                          min_val=0, max_val=1)
            with pool.If(some_outside > 0):
                mean_after = stepper(pool, mean_step)
                mean_after(pool.memset(sums[:], 0.0))
                rows_by_turn = ctx_in.rearrange("(p n) d -> p n d", p=P)
                with pool.Fori(0, MTURN) as turn:
                    pool.dma_start(wide[:], rows_by_turn[:, bass.ds(turn * MROW, MROW), 0:D]
                                   ).then_inc(landed["wide"], 16)
                    pool.wait_ge(landed["wide"], turn * 16 + 16)
                    pool.tensor_tensor(sums[:], sums[:], wide[:], ALU.add).then_inc(done["sums"], 1)
                    pool.wait_ge(done["sums"], turn + 1)
                for n in range(1, MROW):
                    mean_after(pool.tensor_tensor(sums[:, 0], sums[:, 0], sums[:, n], ALU.add))
                mean_after(pool.partition_all_reduce(total[:], sums[:, 0], P, RADD))
                for g in range(NG):
                    pool.wait_ge(landed_key[g], 16)
                    mean_after(pool.tensor_scalar(share[:], total[:], outside[:, g:g + 1], 1.0 / LK,
                                             ALU.mult, ALU.mult))
                    mean_after(pool.tensor_scalar(keys[:, g, 0:D], keys[:, g, 0:D],
                                             inside[:, g:g + 1], None, ALU.mult))
                    mean_after(pool.tensor_tensor(keys[:, g, 0:D], keys[:, g, 0:D], share[:], ALU.add))
            pool.end_ifs()
            pool.memset(share[:, 0:1], 0.0).then_inc(done["keys"], 1)
            for g in range(NG):
                pool.wait_ge(landed_key[g], 16)
            pool.wait_ge(landed["c2"], 16)
            cosk, sink = keys[:, :, D:D + HALF], keys[:, :, D + HALF:D + R]
            pool.tensor_tensor(rt[:, 0], cosk, cosq, ALU.mult)
            pool.tensor_tensor(rt[:, 1], sink, sinq, ALU.mult)
            pool.tensor_tensor(rt[:, 2], sink, cosq, ALU.mult)
            after(pool.tensor_tensor(rt[:, 3], cosk, sinq, ALU.mult))
            pool.tensor_tensor(cosr[:], rt[:, 0], rt[:, 1], ALU.add).then_inc(done["cosr"], 1)
            pool.tensor_tensor(sinr[:], rt[:, 2], rt[:, 3], ALU.subtract).then_inc(done["cosr"], 1)
            pool.wait_ge(done["gate"], 1)
            pool.tensor_copy(gates[:], gate[:].unsqueeze(1).broadcast_to([P, DV, T])).then_inc(
                done["gates"], 1)
            pool.wait_ge(done["eg"], 1)
            pool.tensor_scalar(eg1[0:T, :], eg[0:T, :], 1.0, None, ALU.add).then_inc(done["eg1"], 1)
            pool.wait_ge(done["rg"], 1)
            pool.tensor_tensor(sg[0:T, :], zg[0:T, :], rg[0:T, :], ALU.mult).then_inc(done["sg"], 1)

        @block.scalar
        def _(act):
            after = stepper(act, act_step)
            act.dma_start(x[0:T, :], x_in).then_inc(landed["x"], 16)
            act.preload_act_table_set("natural_log_exp_and_others")
            act.wait_ge(done["consts"], 3)

            def rstd_of(n, eps, variances, ready, signal):
                act.wait_ge(ready, 1)
                after(act.activation(lnv[0:T, n:n + 1], variances, ACT.Ln, bias=eps[0:T, :]))
                act.activation(rstd[0:T, n:n + 1], lnv[0:T, n:n + 1], ACT.Exp,
                               scale=-0.5).then_inc(signal, 1)

            rstd_of(0, eps5, mv[0:T, 0, 1:2], done["mv1"], done["rstd1"])
            act.wait_ge(done["xn1t_ps"], 1)
            act.copy(xn1t[:], bank[0][:, 0:P]).then_inc(done["xn1t"], 1)
            act.wait_ge(done["aq_ps"], 1)
            act.copy(aq[0:QC, 0:HP, 0, :], bank[1][0:QC, :].rearrange("p (h c) -> p h c", c=KVC)).then_inc(done["aq"], 1)
            act.wait_ge(done["kin_ps"], 1)
            act.copy(kt_in[:, :, 0:256].rearrange("p c (g k) -> p g c k", g=2),
                     bank[3][:].rearrange("p (g c k) -> p g c k", g=2, c=DC)).then_inc(done["kin"], 1)
            act.wait_ge(done["kin_ps"], 3)
            act.copy(kt_in[:, :, 512:640],
                     bank[5][:, 0:256].rearrange("p (c k) -> p c k", c=DC)).then_inc(done["kin"], 1)
            act.wait_ge(done["qt_ps"], 1)
            act.copy(qt[:, :, 0:HP, :].rearrange("p c h q -> p h c q"),
                     bank[6][:].rearrange("p (h c q) -> p h c q", h=HP, q=QPC)).then_inc(done["qt"], 1)
            act.wait_ge(done["kv_ps"], 1)
            act.copy(kv[:, 0:4].rearrange("p g s c -> p (g s c)"), bank[1][:]).then_inc(done["kv"], 1)
            act.wait_ge(done["kv_ps"], 2)
            act.copy(kv[:, 4].rearrange("p s c -> p (s c)"), bank[2][:, 0:P]).then_inc(done["kv"], 1)
            act.wait_ge(done["kv"], 2)
            act.copy(kr_[:, :, 0:KVC], kv[:, :, 0, :]).then_inc(done["kr"], 1)
            act.wait_ge(done["kt_ps"], 2)
            act.copy(kt[:, 512:640], bank[4][:, 0:P]).then_inc(done["kt"], 1)
            act.wait_ge(done["vals_ps"], 1)
            act.copy(vals[0:KPC], bank[5][0:KPC, :].rearrange("p (c v) -> p c v", v=KVC)).then_inc(
                done["vals"], 1)
            for c in range(NCH):
                act.wait_ge(done["nmax"], c // 4 + 1)
                act.activation(p[:, c, :], s[:, c, :], ACT.Exp, bias=nmax[:, c:c + 1],
                               accum_out=psums[:, c:c + 1]).then_inc(done["exp"], 1)
            for i in range(HP // 2):
                act.wait_ge(done["wvo_ps"], i + 1)
                act.copy(wvo[:, 2 * i:2 * i + 2, :].rearrange("p h n -> p (h n)"),
                         bank[(6, 7, 0, 4)[i]][:]).then_inc(done["wvo"], 1)

            rstd_of(1, eps5, mv[0:T, 1, 1:2], done["mv2"], done["rstd2"])
            act.wait_ge(done["xn2t_ps"], 1)
            act.copy(xn2t[:], bank[0][:, 0:P]).then_inc(done["xn2t"], 1)
            act.wait_ge(done["v_ps"], 1)
            act.copy(vrep[0:T, 0:8], value_columns(0)).then_inc(done["v"], 1)
            act.wait_ge(done["qk_ps"], 1)
            act.copy(qs[:], bank[4][:, 0:T]).then_inc(done["qs"], 1)
            act.mul(ks[:], bank[4][:, T:2 * T], GK_SCALE).then_inc(done["ks"], 1)
            act.wait_ge(done["nabs"], 1)
            after(act.activation(ez[:], nabs[:], ACT.Exp))
            act.activation(lz[:], ez[:], ACT.Ln, bias=one).then_inc(done["lz"], 1)
            act.wait_ge(done["logsig"], 1)
            act.activation(gate[:, 1:T], logsig[:, 1:T], ACT.Exp, scale=1.0 / GATE_NORM).then_inc(
                done["gate"], 1)
            act.wait_ge(done["zg"], 1)
            act.activation(eg[0:T, :], zg[0:T, :], ACT.Exp, scale=-1.0).then_inc(done["eg"], 1)
            act.wait_ge(done["oc"], 1)
            act.activation(osq[0:T], oc[0:T], ACT.Square).then_inc(done["osq"], 1)
            act.wait_ge(done["ovar"], 1)
            after(act.activation(olnv[0:T, :], ovar[0:T, :], ACT.Ln, bias=eps5[0:T, :],
                                 scale=1.0 / DV))
            act.activation(orstd[0:T, :], olnv[0:T, :], ACT.Exp, scale=-0.5).then_inc(done["orstd"], 1)
            act.wait_ge(done["ogt_ps"], 1)
            act.copy(ogt[:], bank[2][:, 0:P]).then_inc(done["ogt"], 1)

            rstd_of(2, eps5, mv[0:T, 2, 1:2], done["mv3"], done["rstd3"])
            act.wait_ge(done["xn3t_ps"], 1)
            act.copy(xn3t[:], bank[4][:, 0:P]).then_inc(done["xn3t"], 1)
            act.wait_ge(done["gap"], 1)
            act.activation(egap[:], gap[:], ACT.Exp).then_inc(done["egap"], 1)
            act.preload_act_table(ACT.Silu)
            for j in range(2):
                act.wait_ge(done["h"], j + 1)
                act.activation(hs[:, j, :], h[:, j, :], ACT.Silu).then_inc(done["hs"], 1)
            act.preload_act_table_set("natural_log_exp_and_others")
            act.wait_ge(done["combt_ps"], 1)
            act.copy(combt[:], bank[0][:, 0:P]).then_inc(done["combt"], 1)
            act.wait_ge(done["y"], 1)
            after(act.activation(ysq[0:T, :], y[0:T, :], ACT.Square, accum_out=yss[0:T, :]))
            after(act.activation(ylnv[0:T, :], yss[0:T, :], ACT.Ln, bias=eps6[0:T, :],
                                 scale=1.0 / D))
            act.activation(yr[0:T, :], ylnv[0:T, :], ACT.Exp, scale=-0.5).then_inc(done["yr"], 1)

        @block.tensor
        def _(pe):
            def transpose_tokens(src, psum, signal):
                for kc in range(DC):
                    mm = pe.transpose(psum[:, kc * T:(kc + 1) * T],
                                      src[0:T, kc * P:(kc + 1) * P], ident[0:T, 0:T])
                mm.then_inc(signal, 1)

            pe.wait_ge(landed["c2"], 16)
            for kc in range(DC):
                mm = pe.matmul(bank[0][:, 256 + kc * R:256 + (kc + 1) * R],
                               c2_("kvct")[0:KVC, kc * P:(kc + 1) * P], c2_("kr")[0:KVC, :],
                               start=True, stop=True)
            mm.then_inc(done["wkk_ps"], 1)
            pe.wait_ge(landed["c1"], 16)
            pe.wait_ge(done["xn1"], 1)
            pe.wait_ge(done["wkk"], 1)
            transpose_tokens(xn1, bank[0], done["xn1t_ps"])
            pe.wait_ge(done["xn1t"], 1)
            for kc in range(DC):
                mm = pe.matmul(bank[0][0:QC, P:P + T], dq[:, kc, :],
                               xn1t[:, kc * T:(kc + 1) * T], start=kc == 0, stop=kc == DC - 1)
            mm.then_inc(done["qct_ps"], 1)
            pe.wait_ge(landed["uqk"], 16)
            for hh in range(H):
                mm = pe.matmul(bank[1 + hh // HP][0:QC, hh % HP * KVC:(hh % HP + 1) * KVC],
                               uqk[:, hh, 0:QC], uqk[:, hh, QC:], start=True, stop=True)
                if hh % HP == HP - 1:
                    mm.then_inc(done["aq_ps"], 1)
            pe.wait_ge(done["keys"], 1)
            for g in range(NG):
                pe.wait_ge(landed_key[g], 16)
                for kc in range(DC):
                    at = g % 2 * 256 + kc * P
                    mm = pe.transpose(bank[3 + g // 2][:, at:at + P],
                                      keys[:, g, kc * P:(kc + 1) * P], ident)
                if g % 2 == 1 or g == NG - 1:
                    mm.then_inc(done["kin_ps"], 1)
            pe.wait_ge(done["qct"], 1)
            pe.wait_ge(done["aq"], 2)
            pe.wait_ge(landed["qr"], 16)
            for hh in range(H):
                mm = pe.matmul(bank[6 + hh // HP][:, hh % HP * T:(hh % HP + 1) * T],
                               aq[0:QC, hh].rearrange("p s c -> p (s c)"), qct[0:QC, :],
                               start=True, stop=True)
                if hh % HP == HP - 1:
                    mm.then_inc(done["qt_ps"], 1)
            pe.wait_ge(done["kin"], 3)
            for g in range(NG):
                for kc in range(DC):
                    mm = pe.matmul(bank[1 + g // 4][:, g % 4 * P:(g % 4 + 1) * P],
                                   kt_in[:, kc, g * P:(g + 1) * P], kw[:, kc, :],
                                   start=kc == 0, stop=kc == DC - 1)
                if g >= 3:
                    mm.then_inc(done["kv_ps"], 1)
            pe.wait_ge(done["kr"], 3)
            for g in range(NG):
                mm = pe.transpose(bank[3 + g // 4][:, g % 4 * P:(g % 4 + 1) * P], kr_[:, g, :], ident)
                if g >= 3:
                    mm.then_inc(done["kt_ps"], 1)
            pe.wait_ge(done["kt"], 2)
            pe.wait_ge(done["qt"], 2)
            for c in range(NCH):
                mm = pe.matmul(bank[1 + c // 4][:, c % 4 * KPC:(c % 4 + 1) * KPC],
                               qt[:, c].rearrange("p h q -> p (h q)"), kt[:, c * KPC:(c + 1) * KPC],
                               start=True, stop=True)
                if c % 4 == 3:
                    mm.then_inc(done["s_ps"], 1)
            for c in range(NCH):
                mm = pe.transpose(bank[5][0:KPC, c * KVC:(c + 1) * KVC],
                                  kt[0:KVC, c * KPC:(c + 1) * KPC], ident[0:KVC, 0:KVC])
            mm.then_inc(done["vals_ps"], 1)
            pe.wait_ge(landed["uv"], 16)
            for i in range(HP // 2):
                pe.wait_ge(landed_wo[i // 2], 16)
                for hh in range(4 * i, 4 * i + 4):
                    half, at = hh % 2 * KVC, hh // 2 % 2 * D
                    mm = pe.matmul(bank[(6, 7, 0, 4)[i]][half:half + KVC, at:at + D],
                                   uv[:, hh, :], wo[:, hh, :], start=True, stop=True)
                mm.then_inc(done["wvo_ps"], 1)
            for c in range(NCH):
                if c % 4 == 0:
                    pe.wait_ge(done["p"], c // 4 + 1)
                mm = pe.transpose(bank[(3, 1)[c // 4]][0:KPC, c % 4 * P:(c % 4 + 1) * P], p[:, c, :],
                                  ident)
                if c % 4 == 3:
                    mm.then_inc(done["pt_ps"], 1)
            pe.wait_ge(done["vals"], 1)
            for c in range(NCH):
                if c % 4 == 0:
                    pe.wait_ge(done["pt"], c // 4 + 1)
                probs = pt[0:KPC, c, :].rearrange("k (h e q) -> k h e q", e=2, q=QPC)
                for half in range(2):
                    dst = bank[5][half * KVC:(half + 1) * KVC, :].rearrange("v (h t) -> v h t", t=T)
                    mm = pe.matmul(dst[:, :, c * QPC:(c + 1) * QPC], vals[0:KPC, c, :],
                                   probs[:, :, half, :], start=True, stop=True)
            mm.then_inc(done["ctx_ps"], 1)
            pe.wait_ge(done["ctx"], 1)
            pe.wait_ge(done["wvo"], 4)
            for hp in range(HP):
                mm = pe.matmul(bank[2][0:T, 0:D], ctxt[:, hp, :], wvo[:, hp, :],
                               start=hp == 0, stop=hp == HP - 1)
            mm.then_inc(done["y1_ps"], 1)

            pe.wait_ge(done["xn2"], 1)
            transpose_tokens(xn2, bank[0], done["xn2t_ps"])
            pe.wait_ge(done["xn2t"], 1)
            pe.wait_ge(landed["gla"], 16)

            def x_by_token(psum, name):
                for kc in range(DC):
                    mm = pe.matmul(psum, xn2t[:, kc * T:(kc + 1) * T], gla_(kc, name),
                                   start=kc == 0, stop=kc == DC - 1)
                return mm

            def x_by_feature(psum, name):
                for kc in range(DC):
                    mm = pe.matmul(psum, gla_(kc, name), xn2t[:, kc * T:(kc + 1) * T],
                                   start=kc == 0, stop=kc == DC - 1)
                return mm

            x_by_feature(bank[1][0:GLR, 0:T], "kg1").then_inc(done["kg1_ps"], 1)
            for j in range(2):
                for kc in range(DC):
                    wv = gla_(kc, "v").rearrange("p (h v) -> p h v", v=DV)[:, :, 8 * j:8 * j + 8]
                    mm = pe.matmul(bank[2 + j][0:T, 0:P], xn2t[:, kc * T:(kc + 1) * T], wv,
                                   start=kc == 0, stop=kc == DC - 1)
                mm.then_inc(done["v_ps"], 1)
            x_by_feature(bank[4][:, 0:T], "q")
            x_by_feature(bank[4][:, T:2 * T], "k").then_inc(done["qk_ps"], 1)
            pe.wait_ge(done["kg1"], 1)
            pe.wait_ge(landed["kg2"], 16)
            pe.matmul(bank[5][:, 0:T], kg2[0:GLR, 0:P], kg1[0:GLR, :], start=True,
                      stop=True).then_inc(done["kg_ps"], 1)
            pe.wait_ge(done["v"], 2)
            for v in range(DV):
                mm = pe.transpose(bank[6 + v // 8][:, v % 8 * T:(v % 8 + 1) * T],
                                  vrep[0:T, v].rearrange("p h k -> p (h k)"), ident[0:T, 0:T])
                if v % 8 == 7:
                    mm.then_inc(done["vrep_ps"], 1)
            x_by_token(bank[0][0:T, 0:D], "g").then_inc(done["g_ps"], 1)
            for v in range(DV):
                if v % 8 == 0:
                    pe.wait_ge(done["qstate"], v // 8 + 1)
                mm = pe.matmul(bank[1][0:T, v * H:(v + 1) * H], qstate[:, v, :], c2_("headsum"),
                               start=True, stop=True)
            mm.then_inc(done["o_ps"], 1)
            pe.wait_ge(done["og"], 1)
            for kc in range(DC):
                mm = pe.transpose(bank[2][:, kc * T:(kc + 1) * T],
                                  og[0:T].rearrange("p h v -> p (h v)")[:, kc * P:(kc + 1) * P],
                                  ident[0:T, 0:T])
            mm.then_inc(done["ogt_ps"], 1)
            pe.wait_ge(done["ogt"], 1)
            for kc in range(DC):
                mm = pe.matmul(bank[3][0:T, 0:D], ogt[:, kc * T:(kc + 1) * T], gla_(kc, "o"),
                               start=kc == 0, stop=kc == DC - 1)
            mm.then_inc(done["y2_ps"], 1)

            pe.wait_ge(done["xn3"], 1)
            transpose_tokens(xn3, bank[4], done["xn3t_ps"])
            pe.wait_ge(done["xn3t"], 1)
            pe.wait_ge(landed["router"], 16)
            for half in range(2):
                for kc in range(DC):
                    mm = pe.matmul(bank[5][half * T:(half + 1) * T, 0:E],
                                   xn3t[:, kc * T:(kc + 1) * T], router[:, kc, :],
                                   start=kc == 0, stop=kc == DC - 1)
            mm.then_inc(done["lg_ps"], 1)
            for kc in range(DC):
                pe.wait_ge(landed_expert[kc], 16)
            for j in range(2):
                for half in range(2):
                    e = half * EH + 2 * j
                    for kc in range(DC):
                        mm = pe.matmul(bank[6 + j][half * T:(half + 1) * T, :],
                                       xn3t[:, kc * T:(kc + 1) * T],
                                       expert[:, kc, e:e + 2, :].rearrange("p e n -> p (e n)"),
                                       start=kc == 0, stop=kc == DC - 1)
                mm.then_inc(done["h_ps"], 1)
            pe.wait_ge(done["comb"], 1)
            for kc in range(DC):
                mm = pe.matmul(bank[0][:, kc * T:(kc + 1) * T], comb[:, EH - 1, kc * P:(kc + 1) * P],
                               c2_("twice"), start=True, stop=True)
            mm.then_inc(done["combt_ps"], 1)
            pe.wait_ge(done["combt"], 1)
            pe.wait_ge(landed["proj"], 16)
            for kc in range(DC):
                mm = pe.matmul(bank[1][0:T, 0:D], combt[:, kc * T:(kc + 1) * T], proj[:, kc, :],
                               start=kc == 0, stop=kc == DC - 1)
            mm.then_inc(done["y3_ps"], 1)

        @block.vector
        def _(dve):
            after = stepper(dve, dve_step)

            dve.memset(eps5, LN_EPS).then_inc(done["consts"], 1)
            dve.memset(eps6, RMS_EPS).then_inc(done["consts"], 1)
            dve.memset(one, 1.0).then_inc(done["consts"], 1)
            dve.memset(gate[:, 0:1], 0.0).then_inc(done["gates"], 1)

            def moments(n, src, signal):
                after(dve.bn_stats(stats[0:T, n, :], src[0:T, :]))
                dve.bn_aggr(mv[0:T, n, :], stats[0:T, n, :]).then_inc(signal, 1)

            def normalise(n, dst, src, ready, signal):
                dve.wait_ge(ready, 1)
                dve.tensor_scalar(dst[0:T, :], src[0:T, :], mv[0:T, n, 0:1], rstd[0:T, n:n + 1],
                                  ALU.subtract, ALU.mult).then_inc(signal, 1)

            dve.wait_ge(landed["seg"], 16)
            after(dve.tensor_copy(segf[:], seg[:]))
            dve.wait_ge(landed["c1"], 16)
            after(dve.tensor_tensor(kidx[:], segf[:, 0:NG], c1_("koff"), ALU.add))
            dve.tensor_scalar(kidxu[:], kidx[:], 0.0, float(LK - 1), ALU.max, ALU.min).then_inc(
                done["kidx"], 1)
            dve.wait_ge(landed["x"], 16)
            moments(0, x, done["mv1"])
            after(dve.tensor_scalar(segc[:], segf[:], 0.0, float(LK - 1 + LOOKBACK), ALU.max,
                                    ALU.min))
            after(dve.tensor_tensor(inside[:], segc[:], segf[:], ALU.is_equal))
            after(dve.tensor_scalar(outside[:], inside[:, 0:NG], -1.0, 1.0, ALU.mult, ALU.add))
            after(dve.tensor_reduce(lowest[:], inside[:, NG:], AX.X, ALU.min))
            dve.tensor_scalar(flag[:], lowest[:], -1.0, 1.0, ALU.mult, ALU.add).then_inc(
                done["flag"], 1)
            dve.wait_ge(done["mv1"], 1)
            normalise(0, xn1, x, done["rstd1"], done["xn1"])
            after(dve.scalar_tensor_tensor(segv[:], segc[:, NG:], -SHIFT, inside[:, NG:], ALU.add,
                                           ALU.mult))
            after(dve.tensor_tensor(pos[:], segv[:].unsqueeze(2).broadcast_to([P, T, WIN]),
                                    c1_("moff").unsqueeze(1).broadcast_to([P, T, WIN]), ALU.add))
            after(dve.tensor_scalar(posc[:], pos[:], float(LOOKBACK), float(LK - 1 + LOOKBACK),
                                    ALU.max, ALU.min))
            after(dve.tensor_tensor(pos[:], pos[:], posc[:], ALU.not_equal))
            dve.wait_ge(landed["c2"], 16)
            dve.scalar_tensor_tensor(
                maskb[:], pos[:].rearrange("p (c q) m -> p c (q m)", c=NCH), NEG,
                c2_("block").unsqueeze(1).broadcast_to([P, NCH, KPC]), ALU.mult, ALU.add,
            ).then_inc(done["maskb"], 1)
            dve.wait_ge(done["wkk_ps"], 1)
            dve.tensor_copy(kw_kr, bank[0][:, 256:256 + DC * R].rearrange("p (c n) -> p c n", c=DC)
                            ).then_inc(done["wkk"], 1)
            dve.wait_ge(done["qct_ps"], 1)
            dve.tensor_copy(qct[0:QC, :], bank[0][0:QC, P:P + T]).then_inc(done["qct"], 1)
            dve.wait_ge(done["aq_ps"], 2)
            dve.tensor_copy(aq[0:QC, HP:, 0, :],
                            bank[2][0:QC, :].rearrange("p (h c) -> p h c", c=KVC)).then_inc(done["aq"], 1)
            dve.wait_ge(done["kin_ps"], 2)
            dve.tensor_copy(kt_in[:, :, 256:512].rearrange("p c (g k) -> p g c k", g=2),
                            bank[4][:].rearrange("p (g c k) -> p g c k", g=2, c=DC)).then_inc(
                done["kin"], 1)
            dve.wait_ge(done["qt_ps"], 2)
            dve.tensor_copy(qt[:, :, HP:, :].rearrange("p c h q -> p h c q"),
                            bank[7][:].rearrange("p (h c q) -> p h c q", h=HP, q=QPC)).then_inc(
                done["qt"], 1)
            dve.wait_ge(done["cosr"], 2)
            dve.wait_ge(done["kv"], 2)
            krope = kv[:, :, 1, :].rearrange("p g (s r) -> p g s r", s=2)
            dve.tensor_tensor(ru[:], krope, cosr[:].unsqueeze(2).broadcast_to([P, NG, 2, HALF]),
                              ALU.mult)
            after(dve.tensor_tensor(rw[:], krope, sinr[:].unsqueeze(2).broadcast_to([P, NG, 2, HALF]),
                                    ALU.mult))
            dve.tensor_tensor(kr_[:, :, KVC:KVC + HALF], ru[:, :, 0, :], rw[:, :, 1, :],
                              ALU.subtract).then_inc(done["kr"], 1)
            dve.tensor_tensor(kr_[:, :, KVC + HALF:], rw[:, :, 0, :], ru[:, :, 1, :],
                              ALU.add).then_inc(done["kr"], 1)
            dve.wait_ge(done["kt_ps"], 1)
            dve.tensor_copy(kt[:, 0:512], bank[3][:]).then_inc(done["kt"], 1)
            dve.wait_ge(done["maskb"], 1)
            for j in range(2):
                half = slice(4 * j, 4 * j + 4)
                dve.wait_ge(done["s_ps"], j + 1)
                dve.scalar_tensor_tensor(
                    s[:, half, :], bank[1 + j][:, 0:4 * KPC].rearrange("p (c k) -> p c k", k=KPC),
                    QK_SCALE, maskb[:, half, :], ALU.mult, ALU.add).then_inc(done["s"], 1)
                dve.wait_ge(done["s"], j + 1)
                dve.tensor_reduce(nmax[:, half], s[:, half, :], AX.X, ALU.max,
                                  negate=True).then_inc(done["nmax"], 1)
            for j in range(2):
                half = slice(4 * j, 4 * j + 4)
                dve.wait_ge(done["exp"], 4 * j + 4)
                after(dve.reciprocal(rsum[:, half], psums[:, half]))
                dve.tensor_tensor(p[:, half, :], p[:, half, :],
                                  rsum[:, half].unsqueeze(2).broadcast_to([P, 4, KPC]),
                                  ALU.mult).then_inc(done["p"], 1)
            for j in range(2):
                dve.wait_ge(done["pt_ps"], j + 1)
                dve.tensor_copy(pt[0:KPC, 4 * j:4 * j + 4, :].rearrange("k c n -> k (c n)"),
                                bank[(3, 1)[j]][0:KPC, :]).then_inc(done["pt"], 1)
            dve.wait_ge(done["ctx_ps"], 1)
            dve.tensor_copy(ctxt[:].rearrange("p h t -> p (h t)"), bank[5][:]).then_inc(done["ctx"], 1)
            dve.wait_ge(done["y1_ps"], 1)
            dve.tensor_tensor(x1[0:T, :], x[0:T, :], bank[2][0:T, 0:D], ALU.add).then_inc(done["x1"], 1)

            dve.wait_ge(done["x1"], 1)
            moments(1, x1, done["mv2"])
            dve.wait_ge(done["mv2"], 1)
            normalise(1, xn2, x1, done["rstd2"], done["xn2"])
            dve.wait_ge(done["v_ps"], 2)
            dve.tensor_copy(vrep[0:T, 8:16], value_columns(1)).then_inc(done["v"], 1)
            dve.wait_ge(done["kg1_ps"], 1)
            dve.tensor_copy(kg1[0:GLR, :], bank[1][0:GLR, 0:T]).then_inc(done["kg1"], 1)
            dve.wait_ge(done["kg_ps"], 1)
            after(dve.tensor_scalar(z[:], bank[5][:, 0:T], kg2[:, P:P + 1], None, ALU.add))
            dve.scalar_tensor_tensor(nabs[:], z[:], -1.0, z[:], ALU.mult, ALU.min).then_inc(
                done["nabs"], 1)
            after(dve.tensor_scalar(minz[:], z[:], 0.0, None, ALU.min))
            dve.wait_ge(done["lz"], 1)
            dve.tensor_tensor(logsig[:], minz[:], lz[:], ALU.subtract).then_inc(done["logsig"], 1)
            dve.wait_ge(done["ks"], 1)
            for j in range(2):
                dve.wait_ge(done["vrep_ps"], j + 1)
                dve.tensor_tensor(kvt[:, 8 * j:8 * j + 8, :],
                                  bank[6 + j][:].rearrange("p (v t) -> p v t", t=T),
                                  ks[:].unsqueeze(1).broadcast_to([P, 8, T]), ALU.mult).then_inc(
                    done["kvt"], 1)
            dve.wait_ge(done["gates"], 2)
            dve.wait_ge(done["qs"], 1)
            for j in range(2):
                v = slice(8 * j, 8 * j + 8)
                dve.wait_ge(done["kvt"], j + 1)
                after(dve.tensor_tensor_scan(state[:, v, :].rearrange("p v t -> p (v t)"),
                                             gates[:, v, :].rearrange("p v t -> p (v t)"),
                                             kvt[:, v, :].rearrange("p v t -> p (v t)"),
                                             0.0, ALU.mult, ALU.add))
                dve.tensor_tensor(qstate[:, v, :], state[:, v, :],
                                  qs[:].unsqueeze(1).broadcast_to([P, 8, T]), ALU.mult).then_inc(
                    done["qstate"], 1)
            dve.wait_ge(landed["rows"], 16)
            dve.wait_ge(done["g_ps"], 1)
            dve.tensor_tensor(zg[0:T, :], bank[0][0:T, 0:D], rows_("bg"), ALU.add).then_inc(
                done["zg"], 1)
            dve.wait_ge(done["eg1"], 1)
            dve.reciprocal(rg[0:T, :], eg1[0:T, :]).then_inc(done["rg"], 1)
            dve.wait_ge(done["o_ps"], 1)
            o_ps = bank[1][0:T, 0:D].rearrange("p (v h) -> p h v", h=H)
            after(dve.tensor_reduce(osum[0:T, :], o_ps, AX.X, ALU.add))
            dve.scalar_tensor_tensor(oc[0:T], osum[0:T, :].unsqueeze(2).broadcast_to([T, H, DV]),
                                     -1.0 / DV, o_ps, ALU.mult, ALU.add).then_inc(done["oc"], 1)
            dve.wait_ge(done["oc"], 1)
            dve.wait_ge(done["sg"], 1)
            after(dve.tensor_tensor(ocs[0:T], oc[0:T], sg[0:T, :].rearrange("p (h v) -> p h v", h=H),
                                    ALU.mult))
            dve.wait_ge(done["osq"], 1)
            dve.tensor_reduce(ovar[0:T, :], osq[0:T], AX.X, ALU.add).then_inc(done["ovar"], 1)
            dve.wait_ge(done["orstd"], 1)
            dve.tensor_tensor(og[0:T], ocs[0:T], orstd[0:T, :].unsqueeze(2).broadcast_to([T, H, DV]),
                              ALU.mult).then_inc(done["og"], 1)
            dve.wait_ge(done["y2_ps"], 1)
            dve.tensor_tensor(x2[0:T, :], x1[0:T, :], bank[3][0:T, 0:D], ALU.add).then_inc(done["x2"], 1)

            dve.wait_ge(done["x2"], 1)
            moments(2, x2, done["mv3"])
            dve.wait_ge(done["mv3"], 1)
            normalise(2, xn3, x2, done["rstd3"], done["xn3"])
            dve.wait_ge(done["xn3"], 1)
            after(dve.tensor_tensor(xb[0:T, :], xn3[0:T, :], rows_("proj_b"), ALU.add))
            dve.wait_ge(done["lg_ps"], 1)
            after(dve.tensor_tensor(logits[:], bank[5][:, 0:E], rows_("router_b", P), ALU.add))
            after(dve.max(top[:], logits[:]))
            dve.tensor_tensor(gap[:], top[:, 1:2], top[:, 0:1], ALU.subtract).then_inc(done["gap"], 1)
            after(dve.max_index(topi[:], top[:], logits[:]))
            after(dve.tensor_copy(topf[:], topi[:]))
            dve.wait_ge(done["egap"], 1)
            after(dve.tensor_scalar(egap1[:], egap[:], 1.0, None, ALU.add))
            after(dve.reciprocal(w1[:], egap1[:]))
            after(dve.tensor_tensor(w2[:], egap[:], w1[:], ALU.mult))
            dve.wait_ge(landed["c2"], 16)
            dve.tensor_scalar(fw1[:], c2_("iota"), topf[:, 0:1], w1[:], ALU.is_equal, ALU.mult)
            after(dve.tensor_scalar(fw2[:], c2_("iota"), topf[:, 1:2], w2[:], ALU.is_equal, ALU.mult))
            dve.tensor_tensor(fw[0:T, :], fw1[0:T, 0:EH], fw2[0:T, 0:EH], ALU.add)
            after(dve.tensor_tensor(fw[T:, :], fw1[T:, EH:], fw2[T:, EH:], ALU.add))
            dve.wait_ge(landed["expert_b"], 32)
            for j in range(2):
                dve.wait_ge(done["h_ps"], j + 1)
                dve.tensor_tensor(h[:, j, :], bank[6 + j][:],
                                  expert_b[:, j * 2 * D:(j + 1) * 2 * D], ALU.add).then_inc(done["h"], 1)
            for e in range(EH):
                dve.wait_ge(done["hs"], e // 2 + 1)
                part = hs[:, e // 2, e % 2 * D:(e % 2 + 1) * D]
                if e == 0:
                    after(dve.tensor_scalar(comb[:, 0, :], part, fw[:, 0:1], None, ALU.mult))
                elif e < EH - 1:
                    after(dve.scalar_tensor_tensor(comb[:, e, :], part, fw[:, e:e + 1],
                                                   comb[:, e - 1, :], ALU.mult, ALU.add))
                else:
                    dve.scalar_tensor_tensor(comb[:, e, :], part, fw[:, e:e + 1],
                                             comb[:, e - 1, :], ALU.mult, ALU.add).then_inc(
                        done["comb"], 1)
            dve.wait_ge(done["y3_ps"], 1)
            dve.tensor_tensor(y[0:T, :], xb[0:T, :], bank[1][0:T, 0:D], ALU.add).then_inc(done["y"], 1)
            dve.wait_ge(done["yr"], 1)
            after(dve.scalar_tensor_tensor(yn[0:T, :], y[0:T, :], yr[0:T, :], rows_("norm_w"),
                                           ALU.mult, ALU.mult))
            dve.tensor_tensor(fin[0:T, :], yn[0:T, :], x2[0:T, :], ALU.add).then_inc(done["fin"], 1)


def pack(parts, values, rows_=P):
    out = np.zeros((rows_, width(parts)), np.float32)
    for name in parts:
        if name in values:
            a, b = place(parts, name)
            v = values[name]
            out[:v.shape[0], a:a + v.shape[1]] = v
    return out


def by_chunk(w):
    return np.ascontiguousarray(w.reshape(DC, P, -1).transpose(1, 0, 2)).reshape(P, -1)


def rope_tables():
    freq = (1.0 / np.float32(10000.0) ** (np.arange(HALF, dtype=np.float32) / np.float32(HALF))).astype(np.float32)
    ang = (np.arange(LK, dtype=np.float32)[:, None] * freq).astype(np.float32)
    return np.cos(ang).astype(np.float32), np.sin(ang).astype(np.float32)


def kernel(**inputs):
    import concourse.bacc as bacc
    from concourse.bass_utils import run_bass_kernel_spmd

    a = {k: np.asarray(v) for k, v in inputs.items()}
    w = {k[3:]: v for k, v in a.items() if k.startswith("L0_")}
    cos, sin = rope_tables()

    key = np.arange(NG * P) % NKEY
    query = (key // WIN).reshape(NG, P).T
    seg = a["itok_BxS_0_1023"].reshape(T)
    seg_in = np.concatenate([seg[query], np.tile(seg, (P, 1))], axis=1)

    c1 = pack(C1, dict(
        ident=np.eye(P, dtype=np.float32),
        dq=by_chunk(w["xattn_W_dq"]),
        koff=((key % WIN) - LOOKBACK).reshape(NG, P).T,
        moff=np.tile(np.arange(WIN) + SHIFT, (P, 1))))
    own = np.arange(P)[:, None] % QPC == np.arange(KPC)[None, :] // WIN
    kvc = w["xattn_W_kvc"].reshape(DC, P, KVC)
    kw = np.concatenate([kvc, np.zeros_like(kvc)], axis=2).transpose(1, 0, 2).reshape(P, -1)
    c2 = pack(C2, dict(
        kw=kw, kvct=w["xattn_W_kvc"].T, kr=w["xattn_W_kr"],
        block=np.where(own, 0.0, NEG),
        cosq=cos[query].reshape(P, -1), sinq=sin[query].reshape(P, -1),
        headsum=(np.arange(P)[:, None] // DK == np.arange(H)[None, :]),
        twice=np.tile(np.eye(T), (2, 1)), iota=np.tile(np.arange(E), (P, 1))))

    def heads(m, first):
        return m.reshape(first, H, -1)

    uqk = np.concatenate([heads(w["xattn_W_uq"], QC).transpose(2, 1, 0),
                          heads(w["xattn_W_uk"], KVC).transpose(2, 1, 0)], axis=2).reshape(P, -1)
    g = np.concatenate([w[f"attn_{n}"].T.reshape(DC, P, -1)
                        for n in ("Wq", "Wk", "Wkg1", "Wv", "Wg", "Wo")], axis=2)
    kg2 = np.zeros((P, P + 1), np.float32)
    kg2[:GLR, :P] = w["attn_Wkg2"].T
    kg2[:, P] = w["attn_bkg2"]
    arrays = dict(
        seg=seg_in,
        x=a["x"].reshape(T, D),
        c1=c1, c2=c2,
        ctx=np.concatenate([a["ctx_2048"].reshape(LK, D), cos, sin], axis=1),
        uqk=uqk,
        qr=w["xattn_W_qr"],
        uv=heads(w["xattn_W_uv"], KVC).transpose(2, 1, 0).reshape(P, -1),
        wo=w["xattn_W_o"].reshape(H, HD, D).transpose(1, 0, 2).reshape(P, -1),
        gla=g.transpose(1, 0, 2).reshape(P, -1),
        kg2=kg2,
        rows=np.concatenate([w["attn_bg"], w["ffn_proj_b"], w["ffn_norm_w"], w["ffn_router_b"]])[None],
        router=by_chunk(w["ffn_router_w"]),
        expert=w["ffn_expert_w"].reshape(E, DC, P, D).transpose(2, 1, 0, 3).reshape(P, -1),
        expert_b=w["ffn_expert_b"].reshape(2, EH * D),
        proj=by_chunk(w["ffn_proj_w"]))
    arrays = {f"in_{k}": np.ascontiguousarray(v) for k, v in arrays.items()}

    nc = bacc.Bacc("TRN2", target_bir_lowering=False, num_devices=1)
    args = [nc.dram_tensor(k, v.shape, mybir.dt.from_np(v.dtype), kind="ExternalInput").ap()
            for k, v in arrays.items()]
    out = nc.dram_tensor("out", (T, D), F32, kind="ExternalOutput").ap()
    block_kernel(nc, *args, out)
    r = run_bass_kernel_spmd(nc, [arrays], core_ids=[0])
    return r.results[0]["out"].reshape(1, T, D)
```

```python
from contextlib import ExitStack

import numpy as np

import concourse.bass as bass
from concourse import mybir

F32 = mybir.dt.float32
BF16 = mybir.dt.bfloat16
I32 = mybir.dt.int32
U32 = mybir.dt.uint32
ALU = mybir.AluOpType
ACT = mybir.ActivationFunctionType
AX = mybir.AxisListType
RADD = bass.bass_isa.ReduceOp.add

P = 128
T = 64
D = 256
DC = D // P
LK = 6272
H = 16
HP = H // 2
HD = 128
KVC, QC, R = 64, 96, 64
HALF = R // 2
LOOKBACK = 8
WIN = LOOKBACK + 1
NKEY = T * WIN
NG = -(-NKEY // P)
MROW = 7
MTURN = LK // P // MROW
ROW = D + R
QPC = 8
NCH = T // QPC
KPC = QPC * WIN
NEG = -1e30
SHIFT = 1000.0
QK_SCALE = float(1.0 / np.sqrt(np.float32(HD + R)))
LN_EPS = 1e-5
DK, DV = 8, 16
GLR = 16
GK_SCALE = 128.0 ** -0.5
GATE_NORM = 16.0
GLA_EPS = 1e-5
E = 8
EH = E // 2
HPIECES = [[(0, D, 6)], [(0, D, 7)], [(0, D, 0)], [(0, P, 1), (P, D, 4)]]
RMS_EPS = 1e-6

SEG = dict(key=NG, row=T, koff=NG, moff=WIN)
C1 = dict(ident=P, dq=DC * QC)
C2 = dict(kvct=P, kr=R, block=KPC, cosq=NG * HALF, sinq=NG * HALF, headsum=H, twice=T, iota=E,
          kvc=DC * KVC)
UQK_PARTS = 2
WO_PARTS = 4
GLA = dict(q=P, k=P, kg1=GLR, v=D, g=D, o=D)
ROWS = dict(bg=D, proj_b=D, norm_w=D, router_b=E)


def width(parts):
    return sum(parts.values())


def place(parts, name):
    at = 0
    for n, w in parts.items():
        if n == name:
            return at, at + w
        at += w
    raise KeyError(name)


START_DUMMIES = 16


def block_kernel(nc, seg_in, x_in, c1_in, c2_in, ctx_in, uqk_in, qr_in, uv_in, wo_in, gla_in,
                 kg2_in, rows_in, router_in, expert_in, expert_b_in, proj_in, out):
    with ExitStack() as ctx:
        def sb(name, cols, dt=F32, rows=P):
            return ctx.enter_context(nc.sbuf_tensor(name, [rows, *cols], dt))

        def sem(name):
            return ctx.enter_context(nc.semaphore(name))

        bank = [ctx.enter_context(nc.psum_tensor(f"bank{i}", [P, 512], F32)) for i in range(8)]

        seg = sb("seg", [width(SEG)], I32)
        x = sb("x", [D])
        c1 = sb("c1", [width(C1)])
        c2 = sb("c2", [width(C2) + DC * R])
        keys = sb("keys", [NG, ROW])
        uqk = sb("uqk", [H, QC + KVC])
        aq = sb("aq", [H, KVC])
        qr = sb("qr", [H * R])
        uv = sb("uv", [H, KVC])
        wo = sb("wo", [H, D])
        gla = sb("gla", [DC, width(GLA)])
        kg2 = sb("kg2", [P + 1])
        rows = sb("rows", [width(ROWS)])
        router = sb("router", [DC, E])
        expert = sb("expert", [DC, E, D])
        expert_b = sb("expert_b", [EH * D])
        proj = sb("proj", [DC, D])

        def value_columns(j, a, b):
            v = bank[2 + j][0:T, 0:P].rearrange("t (h v) -> t v h", v=8)[:, a:b, :]
            return v.unsqueeze(3).broadcast_to([T, b - a, H, DK])

        def seg_(name):
            a, b = place(SEG, name)
            return segf[:, a:b]

        def c1_(name):
            a, b = place(C1, name)
            return c1[:, a:b]

        def c2_(name):
            a, b = place(C2, name)
            return c2[:, a:b]

        def gla_(kc, name):
            a, b = place(GLA, name)
            return gla[:, kc, a:b]

        def rows_(name, n=T):
            a, b = place(ROWS, name)
            return rows[0:n, a:b]

        ident = c1_("ident")
        kw = c2[:, width(C2) - DC * KVC:].rearrange("p (s c n) -> p c s n", s=2, c=DC)
        dq = c1_("dq").rearrange("p (c n) -> p c n", c=DC)
        cosq = c2_("cosq").rearrange("p (g r) -> p g r", g=NG)
        sinq = c2_("sinq").rearrange("p (g r) -> p g r", g=NG)

        idle = sb("idle", [512], BF16)
        segf = sb("segf", [width(SEG)])
        segc = sb("segc", [NG + T])
        inside = sb("inside", [NG + T])
        outside = sb("outside", [NG])
        lowest = sb("lowest", [1])
        flag = sb("flag", [1], I32)
        kidx = sb("kidx", [NG])
        kidxu = sb("kidxu", [NG], U32)
        segv = sb("segv", [T])
        pos = sb("pos", [T, WIN])
        posc = sb("posc", [T, WIN])
        maskb = sb("maskb", [NCH, KPC])
        wide = sb("wide", [MROW, D])
        sums = sb("sums", [MROW, D])
        total = sb("total", [D])
        share = sb("share", [D])
        consts = sb("consts", [3])
        eps5, eps6, one = consts[:, 0:1], consts[:, 1:2], consts[:, 2:3]
        stats = sb("stats", [4, 6])
        mv = sb("mv", [4, 2])
        lnv = sb("lnv", [4])
        rstd = sb("rstd", [4])
        xn1 = sb("xn1", [D])
        xn1t = sb("xn1t", [DC * T])
        qct = sb("qct", [T])
        qt = sb("qt", [NCH, H, QPC])
        kt_in = sb("kt_in", [DC, NG * P])
        kv = sb("kv", [NG, 2, KVC])
        kr_ = sb("kr_", [NG, 2 * KVC])
        cosr = sb("cosr", [NG, HALF])
        sinr = sb("sinr", [NG, HALF])
        rc = sb("rc", [NG, 2, HALF])
        rs = sb("rs", [NG, 2, HALF])
        ru = sb("ru", [NG, 2, HALF])
        rw = sb("rw", [NG, 2, HALF])
        kt = sb("kt", [NG * P])
        vals = sb("vals", [NCH, KVC])
        s = sb("s", [NCH, KPC])
        nmax = sb("nmax", [NCH])
        p = sb("p", [NCH, KPC])
        psums = sb("psums", [NCH])
        rsum = sb("rsum", [NCH])
        pt = sb("pt", [NCH, P])
        ctxt = sb("ctxt", [HP, T])
        wvo = sb("wvo", [HP, D])
        x1 = sb("x1", [D])

        xn2 = sb("xn2", [D])
        xn2t = sb("xn2t", [DC * T])
        kg1 = sb("kg1", [T])
        z = sb("z", [T])
        nabs = sb("nabs", [T])
        minz = sb("minz", [T])
        ez = sb("ez", [T])
        lz = sb("lz", [T])
        logsig = sb("logsig", [T])
        gates = sb("gates", [DV, T])
        qs = sb("qs", [T])
        ks = sb("ks", [T])
        vrep = sb("vrep", [DV, H, DK])
        kvt = sb("kvt", [DV, T])
        state = sb("state", [DV, T])
        qstate = sb("qstate", [DV, T])
        zg = sb("zg", [D])
        sg = sb("sg", [D])
        wvsum = sb("wvsum", [DC, H])
        wvc = sb("wvc", [DC, H, DV])
        osq = sb("osq", [H, DV])
        ovar = sb("ovar", [H])
        olnv = sb("olnv", [H])
        orstd = sb("orstd", [H])
        ocs = sb("ocs", [H, DV])
        og = sb("og", [H, DV])
        ogt = sb("ogt", [DC * T])
        x2 = sb("x2", [D])

        xn3 = sb("xn3", [D])
        xn3t = sb("xn3t", [DC * T])
        xb = sb("xb", [D])
        logits = sb("logits", [E])
        top = sb("top", [8])
        topi = sb("topi", [8], U32)
        topf = sb("topf", [8])
        gap = sb("gap", [1])
        egap = sb("egap", [1])
        egap1 = sb("egap1", [1])
        w1 = sb("w1", [1])
        w2 = sb("w2", [1])
        fw1 = sb("fw1", [E])
        fw2 = sb("fw2", [E])
        fw = sb("fw", [EH])
        h = state[:].rearrange("p (e v) t -> p e (v t)", e=EH)
        hs = kvt[:].rearrange("p (e v) t -> p e (v t)", e=EH)
        comb = qstate[:].rearrange("p (e v) t -> p e (v t)", e=EH)
        combt = sb("combt", [DC * T])
        y = sb("y", [D])
        ysq = sb("ysq", [D])
        yss = sb("yss", [1])
        ylnv = sb("ylnv", [1])
        yr = sb("yr", [1])
        yn = sb("yn", [D])
        fin = sb("fin", [D])

        landed = {n: sem(f"landed_{n}") for n in (
            "seg", "x", "c1", "c2", "qr", "uv", "gla", "kg2", "rows", "router",
            "expert_b", "proj", "out", "wide")}
        landed_key = [sem(f"landed_key{g}") for g in range(NG)]
        landed_uqk = [sem(f"landed_uqk{i}") for i in range(UQK_PARTS)]
        landed_wo = [sem(f"landed_wo{i}") for i in range(WO_PARTS)]
        landed_expert = [sem(f"landed_expert{i}") for i in range(2)]
        done = {n: sem(f"done_{n}") for n in (
            "consts", "idle", "sums", "kidx", "flag", "keys", "cosr", "maskb",
            "mv1", "rstd1", "xn1", "xn1t_ps", "xn1t", "wkk_ps", "wkk", "qct_ps", "qct",
            "aq_ps", "aq", "kin_ps", "kin_even", "kin_odd", "qt_ps", "qt", "kv_ps", "kv", "kr_c", "kr_r", "kt_ps", "kt",
            "vals_ps", "vals", "s_ps", "s", "nmax", "s_less_max", "exp", "p", "pt_ps", "pt", "wvo_ps", "wvo",
            "ctx_ps", "ctx", "y1_ps", "x1",
            "mv2", "rstd2", "xn2", "xn2t_ps", "xn2t", "kg1_ps", "kg1", "v_ps", "v", "qk_ps",
            "qs", "ks", "kg_ps", "nabs", "lz", "logsig", "gates_start", "gates", "g_ps", "zg", "sg",
            "wvc", "vrep_ps", "kvt", "qstate", "o_ps", "osq", "ovar", "orstd",
            "og", "ogt_ps", "ogt", "y2_ps", "x2",
            "mv3", "rstd3", "xn3", "xn3t_ps", "xn3t", "lg_ps", "gap", "egap", "h_ps", "h",
            "hs", "comb", "combt_ps", "combt", "y3_ps", "y", "yss", "yr", "fin")}
        mean_step = sem("mean_step")
        act_step = sem("act_step")
        dve_step = sem("dve_step")

        def stepper(eng, step_sem):
            count = [0]

            def after(ins):
                count[0] += 1
                ins.then_inc(step_sem, 1)
                eng.wait_ge(step_sem, count[0])
            return after

        block = ctx.enter_context(nc.Block())

        @block.sync
        def _(sp):
            def load(dst, src, signal):
                sp.dma_start(dst, src).then_inc(signal, 16)

            load(seg[:], seg_in, landed["seg"])
            load(c1[:], c1_in, landed["c1"])
            uqk_flat = uqk[:].rearrange("p h n -> p (h n)")
            n = H * (QC + KVC) // UQK_PARTS
            load(uqk_flat[:, 0:n], uqk_in[:, 0:n], landed_uqk[0])
            load(c2[:, 0:width(C2)], c2_in, landed["c2"])
            sp.wait_ge(landed_uqk[0], 16)
            load(uqk_flat[:, n:], uqk_in[:, n:], landed_uqk[1])
            sp.wait_ge(landed["c2"], 16)
            load(qr[0:QC, :], qr_in, landed["qr"])
            sp.wait_ge(landed_uqk[1], 16)
            load(uv[:].rearrange("p h n -> p (h n)"), uv_in, landed["uv"])
            n = H * D // WO_PARTS
            for i in range(WO_PARTS):
                load(wo[:].rearrange("p h n -> p (h n)")[:, i * n:(i + 1) * n],
                     wo_in[:, i * n:(i + 1) * n], landed_wo[i])
            load(gla[:].rearrange("p c n -> p (c n)"), gla_in, landed["gla"])
            load(kg2[:], kg2_in, landed["kg2"])
            load(rows[:], rows_in.broadcast_to([P, width(ROWS)]), landed["rows"])
            load(router[:].rearrange("p c n -> p (c n)"), router_in, landed["router"])
            for g in range(2):
                load(expert_b[g * T:(g + 1) * T, :],
                     expert_b_in[g:g + 1, :].broadcast_to([T, EH * D]), landed["expert_b"])
            for kc in range(DC):
                load(expert[:, kc].rearrange("p e n -> p (e n)"),
                     expert_in[:, kc * E * D:(kc + 1) * E * D], landed_expert[kc])
            load(proj[:].rearrange("p c n -> p (c n)"), proj_in, landed["proj"])
            sp.wait_ge(done["fin"], 1)
            sp.dma_start(out, fin[0:T, :]).then_inc(landed["out"], 16)
            sp.wait_ge(landed["out"], 16)

        @block.gpsimd
        def _(pool):
            pool.wait_ge(done["kidx"], 1)
            for g in range(NG):
                pool.indirect_dma_start(
                    out=keys[:, g, :], out_offset=None, in_=ctx_in,
                    in_offset=bass.IndirectOffsetOnAxis(ap=kidxu[:, g:g + 1], axis=0),
                ).then_inc(landed_key[g], 16)
            pool.wait_ge(done["flag"], 1)
            some_outside = nc.values_load(flag[0:1, 0:1], engines=[mybir.EngineType.Pool],
                                          min_val=0, max_val=1)
            with pool.If(some_outside > 0):
                mean_after = stepper(pool, mean_step)
                mean_after(pool.memset(sums[:], 0.0))
                rows_by_turn = ctx_in.rearrange("(p n) d -> p n d", p=P)
                with pool.Fori(0, MTURN) as turn:
                    pool.dma_start(wide[:], rows_by_turn[:, bass.ds(turn * MROW, MROW), 0:D]
                                   ).then_inc(landed["wide"], 16)
                    pool.wait_ge(landed["wide"], turn * 16 + 16)
                    pool.tensor_tensor(sums[:], sums[:], wide[:], ALU.add).then_inc(done["sums"], 1)
                    pool.wait_ge(done["sums"], turn + 1)
                for n in range(1, MROW):
                    mean_after(pool.tensor_tensor(sums[:, 0], sums[:, 0], sums[:, n], ALU.add))
                mean_after(pool.partition_all_reduce(total[:], sums[:, 0], P, RADD))
                for g in range(NG):
                    pool.wait_ge(landed_key[g], 16)
                    mean_after(pool.tensor_scalar(share[:], total[:], outside[:, g:g + 1], 1.0 / LK,
                                             ALU.mult, ALU.mult))
                    mean_after(pool.tensor_scalar(keys[:, g, 0:D], keys[:, g, 0:D],
                                             inside[:, g:g + 1], None, ALU.mult))
                    mean_after(pool.tensor_tensor(keys[:, g, 0:D], keys[:, g, 0:D], share[:], ALU.add))
            pool.end_ifs()
            pool.memset(share[:, 0:1], 0.0).then_inc(done["keys"], 1)
        @block.scalar
        def _(act):
            after = stepper(act, act_step)
            act.dma_start(x[0:T, :], x_in).then_inc(landed["x"], 16)
            act.preload_act_table_set("natural_log_exp_and_others")
            act.wait_ge(done["consts"], 3)

            def rstd_of(n, eps, variances, ready, signal):
                act.wait_ge(ready, 1)
                after(act.activation(lnv[0:T, n:n + 1], variances, ACT.Ln, bias=eps[0:T, :]))
                act.activation(rstd[0:T, n:n + 1], lnv[0:T, n:n + 1], ACT.Exp,
                               scale=-0.5).then_inc(signal, 1)

            rstd_of(0, eps5, mv[0:T, 0, 1:2], done["mv1"], done["rstd1"])
            act.wait_ge(done["xn1t_ps"], 1)
            act.copy(xn1t[:], bank[0][:, 0:P]).then_inc(done["xn1t"], 1)
            act.wait_ge(done["qct_ps"], 1)
            act.copy(qct[0:QC, :], bank[0][0:QC, P:P + T]).then_inc(done["qct"], 1)
            act.wait_ge(done["aq_ps"], 1)
            act.copy(aq[0:QC, 0:HP, :], bank[1][0:QC, :].rearrange("p (h c) -> p h c", c=KVC)).then_inc(done["aq"], 1)
            act.wait_ge(done["kin_ps"], 1)
            act.copy(kt_in[:, :, 0:256].rearrange("p c (g k) -> p g c k", g=2),
                     bank[3][:].rearrange("p (g c k) -> p g c k", g=2, c=DC)).then_inc(
                done["kin_even"], 1)
            act.wait_ge(done["kin_ps"], 3)
            act.copy(kt_in[:, :, 512:640],
                     bank[5][:, 0:256].rearrange("p (c k) -> p c k", c=DC)).then_inc(
                done["kin_even"], 1)
            act.wait_ge(done["kv_ps"], 1)
            act.copy(kv[:, 0:4].rearrange("p g s c -> p (g s c)"), bank[1][:]).then_inc(done["kv"], 1)
            act.wait_ge(done["kv"], 1)
            act.copy(kr_[:, 0:4, 0:KVC], kv[:, 0:4, 0, :]).then_inc(done["kr_c"], 1)
            act.wait_ge(done["kv_ps"], 2)
            act.copy(kv[:, 4].rearrange("p s c -> p (s c)"), bank[2][:, 0:P]).then_inc(done["kv"], 1)
            act.wait_ge(done["kv"], 2)
            act.copy(kr_[:, 4, 0:KVC], kv[:, 4, 0, :]).then_inc(done["kr_c"], 1)
            act.wait_ge(done["qt_ps"], 1)
            act.copy(qt[:, :, 0:HP, :].rearrange("p c h q -> p h c q"),
                     bank[6][:].rearrange("p (h c q) -> p h c q", h=HP, q=QPC)).then_inc(done["qt"], 1)
            act.wait_ge(done["kt_ps"], 2)
            act.copy(kt[:, 512:640], bank[4][:, 0:P]).then_inc(done["kt"], 1)
            act.wait_ge(done["vals_ps"], 1)
            act.copy(vals[0:KPC], bank[5][0:KPC, :].rearrange("p (c v) -> p c v", v=KVC)).then_inc(
                done["vals"], 1)
            for c in range(NCH // 2):
                act.wait_ge(done["nmax"], 1)
                act.activation(p[:, c, :], s[:, c, :], ACT.Exp, bias=nmax[:, c:c + 1],
                               accum_out=psums[:, c:c + 1]).then_inc(done["exp"], 1)
            act.wait_ge(done["s_less_max"], 1)
            act.activation(p[:, NCH // 2:, :], s[:, NCH // 2:, :], ACT.Exp).then_inc(done["exp"], 1)
            for i in range(HP // 2):
                act.wait_ge(done["wvo_ps"], i + 1)
                act.copy(wvo[:, 2 * i:2 * i + 2, :].rearrange("p h n -> p (h n)"),
                         bank[(6, 7, 0, 4)[i]][:]).then_inc(done["wvo"], 1)

            rstd_of(1, eps5, mv[0:T, 1, 1:2], done["mv2"], done["rstd2"])
            act.wait_ge(done["xn2t_ps"], 1)
            act.copy(xn2t[:], bank[0][:, 0:P]).then_inc(done["xn2t"], 1)
            act.wait_ge(done["v_ps"], 1)
            act.copy(vrep[0:T, 0:8], value_columns(0, 0, 8)).then_inc(done["v"], 1)
            act.wait_ge(done["qk_ps"], 1)
            act.copy(qs[:], bank[4][:, 0:T]).then_inc(done["qs"], 1)
            act.mul(ks[:], bank[4][:, T:2 * T], GK_SCALE).then_inc(done["ks"], 1)
            act.wait_ge(done["nabs"], 1)
            after(act.activation(ez[:], nabs[:], ACT.Exp))
            act.activation(lz[:], ez[:], ACT.Ln, bias=one).then_inc(done["lz"], 1)
            act.wait_ge(done["logsig"], 1)
            for j in range(2):
                act.activation(gates[:, 8 * j:8 * j + 8, 1:T],
                               logsig[:, 1:T].unsqueeze(1).broadcast_to([P, 8, T - 1]), ACT.Exp,
                               scale=1.0 / GATE_NORM).then_inc(done["gates"], 1)
            act.preload_act_table(ACT.Silu)
            act.wait_ge(done["zg"], 1)
            act.activation(sg[0:T, :], zg[0:T, :], ACT.Silu).then_inc(done["sg"], 1)
            act.preload_act_table_set("natural_log_exp_and_others")
            act.wait_ge(done["o_ps"], 1)
            act.activation(osq[0:T], bank[1][0:T, 0:D].rearrange("p (v h) -> p h v", h=H),
                           ACT.Square).then_inc(done["osq"], 1)
            act.wait_ge(done["ovar"], 1)
            after(act.activation(olnv[0:T, :], ovar[0:T, :], ACT.Ln, bias=eps5[0:T, :],
                                 scale=1.0 / DV))
            act.activation(orstd[0:T, :], olnv[0:T, :], ACT.Exp, scale=-0.5).then_inc(done["orstd"], 1)
            act.wait_ge(done["ogt_ps"], 1)
            act.copy(ogt[:], bank[2][:, 0:P]).then_inc(done["ogt"], 1)

            rstd_of(2, eps5, mv[0:T, 2, 1:2], done["mv3"], done["rstd3"])
            act.wait_ge(done["xn3t_ps"], 1)
            act.copy(xn3t[:], bank[4][:, 0:P]).then_inc(done["xn3t"], 1)
            act.wait_ge(done["gap"], 1)
            act.activation(egap[:], gap[:], ACT.Exp).then_inc(done["egap"], 1)
            act.preload_act_table(ACT.Silu)
            n = 0
            for e in range(EH):
                for a, b, _ in HPIECES[e]:
                    n += 1
                    act.wait_ge(done["h"], n)
                    act.activation(hs[:, e, a:b], h[:, e, a:b], ACT.Silu).then_inc(done["hs"], 1)
            act.preload_act_table_set("natural_log_exp_and_others")
            act.wait_ge(done["combt_ps"], 1)
            act.copy(combt[:], bank[2][:, 0:P]).then_inc(done["combt"], 1)
            act.wait_ge(done["y"], 1)
            after(act.activation(ysq[0:T, :], y[0:T, :], ACT.Square, accum_out=yss[0:T, :]))
            after(act.activation(ylnv[0:T, :], yss[0:T, :], ACT.Ln, bias=eps6[0:T, :],
                                 scale=1.0 / D))
            act.activation(yr[0:T, :], ylnv[0:T, :], ACT.Exp, scale=-0.5).then_inc(done["yr"], 1)

        @block.tensor
        def _(pe):
            def transpose_tokens(src, psum, signal):
                for kc in range(DC):
                    mm = pe.transpose(psum[:, kc * T:(kc + 1) * T],
                                      src[0:T, kc * P:(kc + 1) * P], ident[0:T, 0:T])
                mm.then_inc(signal, 1)

            def keep_clock(n, psum):
                for _ in range(n):
                    pe.matmul(psum[:], idle[:, 0:P], idle[:], start=True, stop=True)

            pe.wait_ge(done["idle"], 1)
            keep_clock(START_DUMMIES, bank[7])
            pe.wait_ge(landed["c1"], 16)
            pe.wait_ge(done["xn1"], 1)
            transpose_tokens(xn1, bank[0], done["xn1t_ps"])
            pe.wait_ge(done["xn1t"], 1)
            for kc in range(DC):
                mm = pe.matmul(bank[0][0:QC, P:P + T], dq[:, kc, :],
                               xn1t[:, kc * T:(kc + 1) * T], start=kc == 0, stop=kc == DC - 1)
            mm.then_inc(done["qct_ps"], 1)

            def fold_uk(j):
                pe.wait_ge(landed_uqk[j], 16)
                for i in range(HP):
                    hh = j * HP + i
                    mm = pe.matmul(bank[1 + j][0:QC, i * KVC:(i + 1) * KVC],
                                   uqk[:, hh, 0:QC], uqk[:, hh, QC:], start=True, stop=True)
                mm.then_inc(done["aq_ps"], 1)

            def transpose_keys(g):
                pe.wait_ge(landed_key[g], 16)
                for kc in range(DC):
                    at = g % 2 * 256 + kc * P
                    mm = pe.transpose(bank[3 + g // 2][:, at:at + P],
                                      keys[:, g, kc * P:(kc + 1) * P], ident)
                if g % 2 == 1 or g == NG - 1:
                    mm.then_inc(done["kin_ps"], 1)

            def project_keys(g):
                pe.wait_ge(done["kin_odd" if g // 2 == 1 else "kin_even"], g // 4 + 1)
                for kc in range(DC):
                    mm = pe.matmul(bank[1 + g // 4][:, g % 4 * P:(g % 4 + 1) * P],
                                   kt_in[:, kc, g * P:(g + 1) * P], kw[:, kc],
                                   start=kc == 0, stop=kc == DC - 1)
                if g >= 3:
                    mm.then_inc(done["kv_ps"], 1)

            fold_uk(0)
            pe.wait_ge(landed["c2"], 16)
            pe.wait_ge(done["qct"], 1)
            for kc in range(DC):
                half = slice(kc * KVC, (kc + 1) * KVC)
                pe.matmul(bank[5 * kc][:, 256:256 + R], c2_("kvct")[half, :], c2_("kr")[half, :],
                          start=True, stop=True).then_inc(done["wkk_ps"], 1)
            pe.wait_ge(done["keys"], 1)
            transpose_keys(0)
            transpose_keys(1)
            fold_uk(1)
            transpose_keys(2)
            transpose_keys(3)
            pe.wait_ge(done["wkk"], 2)
            transpose_keys(4)
            pe.wait_ge(landed["qr"], 16)
            for hh in range(H):
                pe.matmul(bank[6 + hh // HP][KVC:P, hh % HP * T:(hh % HP + 1) * T],
                          qr[0:QC, hh * R:(hh + 1) * R], qct[0:QC, :], start=True, stop=True)
            pe.wait_ge(done["aq"], 2)
            for g in range(NG):
                project_keys(g)
            for hh in range(H):
                mm = pe.matmul(bank[6 + hh // HP][0:KVC, hh % HP * T:(hh % HP + 1) * T],
                               aq[0:QC, hh, :], qct[0:QC, :], start=True, stop=True)
                if hh % HP == HP - 1:
                    mm.then_inc(done["qt_ps"], 1)
            for g in range(NG):
                pe.wait_ge(done["kr_c"], g // 4 + 1)
                pe.wait_ge(done["kr_r"], 2 * (g // 4 + 1))
                mm = pe.transpose(bank[3 + g // 4][:, g % 4 * P:(g % 4 + 1) * P], kr_[:, g, :], ident)
                if g >= 3:
                    mm.then_inc(done["kt_ps"], 1)
            pe.wait_ge(done["kt"], 2)
            pe.wait_ge(done["qt"], 2)
            for c in range(NCH):
                mm = pe.matmul(bank[1 + c // 4][:, c % 4 * KPC:(c % 4 + 1) * KPC],
                               qt[:, c].rearrange("p h q -> p (h q)"), kt[:, c * KPC:(c + 1) * KPC],
                               start=True, stop=True)
                if c % 4 == 3:
                    mm.then_inc(done["s_ps"], 1)
            for c in range(NCH):
                mm = pe.transpose(bank[5][0:KPC, c * KVC:(c + 1) * KVC],
                                  kt[0:KVC, c * KPC:(c + 1) * KPC], ident[0:KVC, 0:KVC])
            mm.then_inc(done["vals_ps"], 1)
            pe.wait_ge(landed["uv"], 16)
            for i in range(HP // 2):
                pe.wait_ge(landed_wo[i], 16)
                for hh in range(4 * i, 4 * i + 4):
                    half, at = hh % 2 * KVC, hh // 2 % 2 * D
                    mm = pe.matmul(bank[(6, 7, 0, 4)[i]][half:half + KVC, at:at + D],
                                   uv[:, hh, :], wo[:, hh, :], start=True, stop=True)
                mm.then_inc(done["wvo_ps"], 1)
            for c in range(NCH):
                if c % 4 == 0:
                    pe.wait_ge(done["p"], c // 4 + 1)
                mm = pe.transpose(bank[(3, 1)[c // 4]][0:KPC, c % 4 * P:(c % 4 + 1) * P], p[:, c, :],
                                  ident)
                if c % 4 == 3:
                    mm.then_inc(done["pt_ps"], 1)
            pe.wait_ge(done["vals"], 1)
            for c in range(NCH):
                if c % 4 == 0:
                    pe.wait_ge(done["pt"], c // 4 + 1)
                probs = pt[0:KPC, c, :].rearrange("k (h e q) -> k h e q", e=2, q=QPC)
                for half in range(2):
                    dst = bank[5][half * KVC:(half + 1) * KVC, :].rearrange("v (h t) -> v h t", t=T)
                    mm = pe.matmul(dst[:, :, c * QPC:(c + 1) * QPC], vals[0:KPC, c, :],
                                   probs[:, :, half, :], start=True, stop=True)
            mm.then_inc(done["ctx_ps"], 1)
            pe.wait_ge(done["ctx"], 1)
            pe.wait_ge(done["wvo"], 4)
            for hp in range(HP):
                mm = pe.matmul(bank[2][0:T, 0:D], ctxt[:, hp, :], wvo[:, hp, :],
                               start=hp == 0, stop=hp == HP - 1)
            mm.then_inc(done["y1_ps"], 1)

            keep_clock(8, bank[7])
            pe.wait_ge(done["xn2"], 1)
            transpose_tokens(xn2, bank[0], done["xn2t_ps"])
            keep_clock(1, bank[7])
            pe.wait_ge(done["xn2t"], 1)
            pe.wait_ge(landed["gla"], 16)

            def x_by_token(psum, name):
                for kc in range(DC):
                    mm = pe.matmul(psum, xn2t[:, kc * T:(kc + 1) * T], gla_(kc, name),
                                   start=kc == 0, stop=kc == DC - 1)
                return mm

            def x_by_feature(psum, name):
                for kc in range(DC):
                    mm = pe.matmul(psum, gla_(kc, name), xn2t[:, kc * T:(kc + 1) * T],
                                   start=kc == 0, stop=kc == DC - 1)
                return mm

            x_by_feature(bank[1][0:GLR, 0:T], "kg1").then_inc(done["kg1_ps"], 1)
            pe.wait_ge(done["wvc"], 2)
            for j in range(2):
                for kc in range(DC):
                    mm = pe.matmul(bank[2 + j][0:T, 0:P], xn2t[:, kc * T:(kc + 1) * T],
                                   wvc[:, kc, :, 8 * j:8 * j + 8],
                                   start=kc == 0, stop=kc == DC - 1)
                mm.then_inc(done["v_ps"], 1)
            x_by_feature(bank[4][:, 0:T], "q")
            x_by_feature(bank[4][:, T:2 * T], "k").then_inc(done["qk_ps"], 1)
            pe.wait_ge(done["kg1"], 1)
            pe.wait_ge(landed["kg2"], 16)
            pe.matmul(bank[5][:, 0:T], kg2[0:GLR, 0:P], kg1[0:GLR, :], start=True,
                      stop=True).then_inc(done["kg_ps"], 1)
            x_by_token(bank[0][0:T, 0:D], "g").then_inc(done["g_ps"], 1)
            keep_clock(1, bank[7])
            pe.wait_ge(done["v"], 3)
            for v in range(DV):
                mm = pe.transpose(bank[6 + v // 8][:, v % 8 * T:(v % 8 + 1) * T],
                                  vrep[0:T, v].rearrange("p h k -> p (h k)"), ident[0:T, 0:T])
                if v % 8 == 7:
                    mm.then_inc(done["vrep_ps"], 1)
            keep_clock(8, bank[5])
            for v in range(DV):
                if v % 8 == 0:
                    pe.wait_ge(done["qstate"], v // 8 + 1)
                mm = pe.matmul(bank[1][0:T, v * H:(v + 1) * H], qstate[:, v, :], c2_("headsum"),
                               start=True, stop=True)
            mm.then_inc(done["o_ps"], 1)
            keep_clock(9, bank[5])
            pe.wait_ge(done["og"], 1)
            for kc in range(DC):
                mm = pe.transpose(bank[2][:, kc * T:(kc + 1) * T],
                                  og[0:T].rearrange("p h v -> p (h v)")[:, kc * P:(kc + 1) * P],
                                  ident[0:T, 0:T])
            mm.then_inc(done["ogt_ps"], 1)
            keep_clock(1, bank[5])
            pe.wait_ge(done["ogt"], 1)
            for kc in range(DC):
                mm = pe.matmul(bank[3][0:T, 0:D], ogt[:, kc * T:(kc + 1) * T], gla_(kc, "o"),
                               start=kc == 0, stop=kc == DC - 1)
            mm.then_inc(done["y2_ps"], 1)

            keep_clock(8, bank[5])
            pe.wait_ge(done["xn3"], 1)
            transpose_tokens(xn3, bank[4], done["xn3t_ps"])
            keep_clock(1, bank[5])
            pe.wait_ge(done["xn3t"], 1)
            pe.wait_ge(landed["router"], 16)
            for half in range(2):
                for kc in range(DC):
                    mm = pe.matmul(bank[5][half * T:(half + 1) * T, 0:E],
                                   xn3t[:, kc * T:(kc + 1) * T], router[:, kc, :],
                                   start=kc == 0, stop=kc == DC - 1)
            mm.then_inc(done["lg_ps"], 1)
            for kc in range(DC):
                pe.wait_ge(landed_expert[kc], 16)
            for e in range(EH):
                for a, b, psum in HPIECES[e]:
                    for half in range(2):
                        for kc in range(DC):
                            mm = pe.matmul(bank[psum][half * T:(half + 1) * T, a:b],
                                           xn3t[:, kc * T:(kc + 1) * T],
                                           expert[:, kc, half * EH + e, a:b],
                                           start=kc == 0, stop=kc == DC - 1)
                    mm.then_inc(done["h_ps"], 1)
            keep_clock(4, bank[3])
            for kc in range(DC):
                pe.wait_ge(done["comb"], EH + kc)
                mm = pe.matmul(bank[2][:, kc * T:(kc + 1) * T], comb[:, EH - 1, kc * P:(kc + 1) * P],
                               c2_("twice"), start=True, stop=True)
            mm.then_inc(done["combt_ps"], 1)
            keep_clock(1, bank[3])
            pe.wait_ge(done["combt"], 1)
            pe.wait_ge(landed["proj"], 16)
            for kc in range(DC):
                mm = pe.matmul(bank[3][0:T, 0:D], combt[:, kc * T:(kc + 1) * T], proj[:, kc, :],
                               start=kc == 0, stop=kc == DC - 1)
            mm.then_inc(done["y3_ps"], 1)

        @block.vector
        def _(dve):
            after = stepper(dve, dve_step)

            dve.memset(eps5, LN_EPS).then_inc(done["consts"], 1)
            dve.memset(eps6, RMS_EPS).then_inc(done["consts"], 1)
            dve.memset(one, 1.0).then_inc(done["consts"], 1)
            dve.memset(idle[:], 0.0).then_inc(done["idle"], 1)

            def moments(n, src, signal):
                after(dve.bn_stats(stats[0:T, n, :], src[0:T, :]))
                dve.bn_aggr(mv[0:T, n, :], stats[0:T, n, :]).then_inc(signal, 1)

            def normalise(n, dst, src, ready, signal):
                dve.wait_ge(ready, 1)
                dve.tensor_scalar(dst[0:T, :], src[0:T, :], mv[0:T, n, 0:1], rstd[0:T, n:n + 1],
                                  ALU.subtract, ALU.mult).then_inc(signal, 1)

            def spread(per_chunk):
                return per_chunk.unsqueeze(2).broadcast_to([P, NCH // 2, KPC])

            dve.wait_ge(landed["seg"], 16)
            after(dve.tensor_copy(segf[:], seg[:]))
            after(dve.tensor_tensor(kidx[:], seg_("key"), seg_("koff"), ALU.add))
            dve.tensor_scalar(kidxu[:], kidx[:], 0.0, float(LK - 1), ALU.max, ALU.min).then_inc(
                done["kidx"], 1)
            dve.wait_ge(landed["x"], 16)
            moments(0, x, done["mv1"])
            after(dve.tensor_scalar(segc[:], segf[:, 0:NG + T], 0.0, float(LK - 1 + LOOKBACK), ALU.max,
                                    ALU.min))
            after(dve.tensor_tensor(inside[:], segc[:], segf[:, 0:NG + T], ALU.is_equal))
            after(dve.tensor_scalar(outside[:], inside[:, 0:NG], -1.0, 1.0, ALU.mult, ALU.add))
            after(dve.tensor_reduce(lowest[:], inside[:, NG:], AX.X, ALU.min))
            dve.tensor_scalar(flag[:], lowest[:], -1.0, 1.0, ALU.mult, ALU.add).then_inc(
                done["flag"], 1)
            dve.wait_ge(done["mv1"], 1)
            normalise(0, xn1, x, done["rstd1"], done["xn1"])
            after(dve.scalar_tensor_tensor(segv[:], segc[:, NG:], -SHIFT, inside[:, NG:], ALU.add,
                                           ALU.mult))
            after(dve.tensor_tensor(pos[:], segv[:].unsqueeze(2).broadcast_to([P, T, WIN]),
                                    seg_("moff").unsqueeze(1).broadcast_to([P, T, WIN]), ALU.add))
            after(dve.tensor_scalar(posc[:], pos[:], float(LOOKBACK), float(LK - 1 + LOOKBACK),
                                    ALU.max, ALU.min))
            after(dve.tensor_tensor(pos[:], pos[:], posc[:], ALU.not_equal))
            dve.memset(gates[:, :, 0:1], 0.0).then_inc(done["gates_start"], 1)
            for kc in range(DC):
                dve.wait_ge(done["wkk_ps"], kc + 1)
                dve.tensor_copy(kw[:, kc, 1, :], bank[5 * kc][:, 256:256 + R]).then_inc(
                    done["wkk"], 1)
            dve.scalar_tensor_tensor(
                maskb[:], pos[:].rearrange("p (c q) m -> p c (q m)", c=NCH), NEG,
                c2_("block").unsqueeze(1).broadcast_to([P, NCH, KPC]), ALU.mult, ALU.add,
            ).then_inc(done["maskb"], 1)
            dve.wait_ge(done["aq_ps"], 2)
            dve.tensor_copy(aq[0:QC, HP:, :],
                            bank[2][0:QC, :].rearrange("p (h c) -> p h c", c=KVC)).then_inc(
                done["aq"], 1)
            dve.wait_ge(done["kin_ps"], 2)
            dve.tensor_copy(kt_in[:, :, 256:512].rearrange("p c (g k) -> p g c k", g=2),
                            bank[4][:].rearrange("p (g c k) -> p g c k", g=2, c=DC)).then_inc(
                done["kin_odd"], 1)
            for g in range(NG):
                dve.wait_ge(landed_key[g], 16)
            both = keys[:, :, D:D + R].rearrange("p g (s r) -> p g s r", s=2)
            dve.tensor_tensor(rc[:], both, cosq.unsqueeze(2).broadcast_to([P, NG, 2, HALF]), ALU.mult)
            after(dve.tensor_tensor(rs[:], both, sinq.unsqueeze(2).broadcast_to([P, NG, 2, HALF]),
                                    ALU.mult))
            dve.tensor_tensor(cosr[:], rc[:, :, 0, :], rs[:, :, 1, :], ALU.add).then_inc(done["cosr"], 1)
            dve.tensor_tensor(sinr[:], rc[:, :, 1, :], rs[:, :, 0, :], ALU.subtract).then_inc(
                done["cosr"], 1)
            dve.wait_ge(done["cosr"], 2)
            for j, part in enumerate((slice(0, 4), slice(4, NG))):
                n = part.stop - part.start
                dve.wait_ge(done["kv"], j + 1)
                krope = kv[:, part, 1, :].rearrange("p g (s r) -> p g s r", s=2)
                dve.tensor_tensor(ru[:, part], krope,
                                  cosr[:, part].unsqueeze(2).broadcast_to([P, n, 2, HALF]), ALU.mult)
                after(dve.tensor_tensor(rw[:, part], krope,
                                        sinr[:, part].unsqueeze(2).broadcast_to([P, n, 2, HALF]),
                                        ALU.mult))
                dve.tensor_tensor(kr_[:, part, KVC:KVC + HALF], ru[:, part, 0, :], rw[:, part, 1, :],
                                  ALU.subtract).then_inc(done["kr_r"], 1)
                dve.tensor_tensor(kr_[:, part, KVC + HALF:], rw[:, part, 0, :], ru[:, part, 1, :],
                                  ALU.add).then_inc(done["kr_r"], 1)
            dve.wait_ge(done["qt_ps"], 2)
            dve.tensor_copy(qt[:, :, HP:, :].rearrange("p c h q -> p h c q"),
                            bank[7][:].rearrange("p (h c q) -> p h c q", h=HP, q=QPC)).then_inc(
                done["qt"], 1)
            dve.wait_ge(done["kt_ps"], 1)
            dve.tensor_copy(kt[:, 0:512], bank[3][:]).then_inc(done["kt"], 1)
            dve.wait_ge(done["maskb"], 1)
            first, second = slice(0, NCH // 2), slice(NCH // 2, NCH)
            for j, half in enumerate((first, second)):
                dve.wait_ge(done["s_ps"], j + 1)
                dve.scalar_tensor_tensor(
                    s[:, half, :], bank[1 + j][:, 0:4 * KPC].rearrange("p (c k) -> p c k", k=KPC),
                    QK_SCALE, maskb[:, half, :], ALU.mult, ALU.add).then_inc(done["s"], 1)
                dve.wait_ge(done["s"], j + 1)
                dve.tensor_reduce(nmax[:, half], s[:, half, :], AX.X, ALU.max,
                                  negate=True).then_inc(done["nmax"], 1)
            dve.wait_ge(done["nmax"], 2)
            dve.tensor_tensor(s[:, second, :], s[:, second, :], spread(nmax[:, second]),
                              ALU.add).then_inc(done["s_less_max"], 1)
            dve.wait_ge(done["exp"], NCH // 2)
            after(dve.reciprocal(rsum[:, first], psums[:, first]))
            dve.tensor_tensor(p[:, first, :], p[:, first, :], spread(rsum[:, first]),
                              ALU.mult).then_inc(done["p"], 1)
            dve.wait_ge(done["exp"], NCH // 2 + 1)
            after(dve.tensor_reduce(psums[:, second], p[:, second, :], AX.X, ALU.add))
            after(dve.reciprocal(rsum[:, second], psums[:, second]))
            dve.tensor_tensor(p[:, second, :], p[:, second, :], spread(rsum[:, second]),
                              ALU.mult).then_inc(done["p"], 1)
            for j in range(2):
                dve.wait_ge(done["pt_ps"], j + 1)
                dve.tensor_copy(pt[0:KPC, 4 * j:4 * j + 4, :].rearrange("k c n -> k (c n)"),
                                bank[(3, 1)[j]][0:KPC, :]).then_inc(done["pt"], 1)
            dve.wait_ge(done["ctx_ps"], 1)
            dve.tensor_copy(ctxt[:].rearrange("p h t -> p (h t)"), bank[5][:]).then_inc(done["ctx"], 1)
            dve.wait_ge(landed["gla"], 16)
            a, b = place(GLA, "v")
            after(dve.tensor_reduce(wvsum[:], gla[:, :, a:b].rearrange("p c (h v) -> p c h v", v=DV),
                                    AX.X, ALU.add))
            for kc in range(DC):
                dve.scalar_tensor_tensor(wvc[:, kc], wvsum[:, kc].unsqueeze(2).broadcast_to([P, H, DV]),
                                         -1.0 / DV, gla_(kc, "v").rearrange("p (h v) -> p h v", v=DV),
                                         ALU.mult, ALU.add).then_inc(done["wvc"], 1)
            dve.wait_ge(done["y1_ps"], 1)
            dve.tensor_tensor(x1[0:T, :], x[0:T, :], bank[2][0:T, 0:D], ALU.add).then_inc(done["x1"], 1)

            dve.wait_ge(done["x1"], 1)
            moments(1, x1, done["mv2"])
            dve.wait_ge(done["mv2"], 1)
            normalise(1, xn2, x1, done["rstd2"], done["xn2"])
            dve.wait_ge(done["kg1_ps"], 1)
            dve.tensor_copy(kg1[0:GLR, :], bank[1][0:GLR, 0:T]).then_inc(done["kg1"], 1)
            dve.wait_ge(done["v_ps"], 2)
            dve.tensor_copy(vrep[0:T, 8:12], value_columns(1, 0, 4)).then_inc(done["v"], 1)
            dve.wait_ge(done["kg_ps"], 1)
            after(dve.tensor_scalar(z[:], bank[5][:, 0:T], kg2[:, P:P + 1], None, ALU.add))
            dve.scalar_tensor_tensor(nabs[:], z[:], -1.0, z[:], ALU.mult, ALU.min).then_inc(
                done["nabs"], 1)
            after(dve.tensor_scalar(minz[:], z[:], 0.0, None, ALU.min))
            dve.tensor_copy(vrep[0:T, 12:16], value_columns(1, 4, 8)).then_inc(done["v"], 1)
            dve.wait_ge(done["lz"], 1)
            dve.tensor_tensor(logsig[:], minz[:], lz[:], ALU.subtract).then_inc(done["logsig"], 1)
            dve.wait_ge(done["ks"], 1)
            for j in range(2):
                dve.wait_ge(done["vrep_ps"], j + 1)
                dve.tensor_tensor(kvt[:, 8 * j:8 * j + 8, :],
                                  bank[6 + j][:].rearrange("p (v t) -> p v t", t=T),
                                  ks[:].unsqueeze(1).broadcast_to([P, 8, T]), ALU.mult).then_inc(
                    done["kvt"], 1)
            dve.wait_ge(landed["rows"], 16)
            dve.wait_ge(done["g_ps"], 1)
            dve.tensor_tensor(zg[0:T, :], bank[0][0:T, 0:D], rows_("bg"), ALU.add).then_inc(
                done["zg"], 1)
            dve.wait_ge(done["qs"], 1)
            dve.wait_ge(done["gates_start"], 1)
            for j in range(2):
                v = slice(8 * j, 8 * j + 8)
                dve.wait_ge(done["kvt"], j + 1)
                dve.wait_ge(done["gates"], j + 1)
                after(dve.tensor_tensor_scan(state[:, v, :].rearrange("p v t -> p (v t)"),
                                             gates[:, v, :].rearrange("p v t -> p (v t)"),
                                             kvt[:, v, :].rearrange("p v t -> p (v t)"),
                                             0.0, ALU.mult, ALU.add))
                dve.tensor_tensor(qstate[:, v, :], state[:, v, :],
                                  qs[:].unsqueeze(1).broadcast_to([P, 8, T]), ALU.mult).then_inc(
                    done["qstate"], 1)
            dve.wait_ge(done["osq"], 1)
            dve.tensor_reduce(ovar[0:T, :], osq[0:T], AX.X, ALU.add).then_inc(done["ovar"], 1)
            dve.wait_ge(done["sg"], 1)
            after(dve.tensor_tensor(ocs[0:T], bank[1][0:T, 0:D].rearrange("p (v h) -> p h v", h=H),
                                    sg[0:T, :].rearrange("p (h v) -> p h v", h=H), ALU.mult))
            dve.wait_ge(done["orstd"], 1)
            dve.tensor_tensor(og[0:T], ocs[0:T], orstd[0:T, :].unsqueeze(2).broadcast_to([T, H, DV]),
                              ALU.mult).then_inc(done["og"], 1)
            dve.wait_ge(done["y2_ps"], 1)
            dve.tensor_tensor(x2[0:T, :], x1[0:T, :], bank[3][0:T, 0:D], ALU.add).then_inc(done["x2"], 1)

            dve.wait_ge(done["x2"], 1)
            moments(2, x2, done["mv3"])
            dve.wait_ge(done["mv3"], 1)
            normalise(2, xn3, x2, done["rstd3"], done["xn3"])
            dve.wait_ge(done["xn3"], 1)
            after(dve.tensor_tensor(xb[0:T, :], xn3[0:T, :], rows_("proj_b"), ALU.add))
            dve.wait_ge(done["lg_ps"], 1)
            after(dve.tensor_tensor(logits[:], bank[5][:, 0:E], rows_("router_b", P), ALU.add))
            after(dve.max(top[:], logits[:]))
            dve.tensor_tensor(gap[:], top[:, 1:2], top[:, 0:1], ALU.subtract).then_inc(done["gap"], 1)
            after(dve.max_index(topi[:], top[:], logits[:]))
            after(dve.tensor_copy(topf[:], topi[:]))
            dve.wait_ge(done["egap"], 1)
            after(dve.tensor_scalar(egap1[:], egap[:], 1.0, None, ALU.add))
            after(dve.reciprocal(w1[:], egap1[:]))
            after(dve.tensor_tensor(w2[:], egap[:], w1[:], ALU.mult))
            dve.wait_ge(landed["c2"], 16)
            dve.tensor_scalar(fw1[:], c2_("iota"), topf[:, 0:1], w1[:], ALU.is_equal, ALU.mult)
            after(dve.tensor_scalar(fw2[:], c2_("iota"), topf[:, 1:2], w2[:], ALU.is_equal, ALU.mult))
            dve.tensor_tensor(fw[0:T, :], fw1[0:T, 0:EH], fw2[0:T, 0:EH], ALU.add)
            after(dve.tensor_tensor(fw[T:, :], fw1[T:, EH:], fw2[T:, EH:], ALU.add))
            dve.wait_ge(landed["expert_b"], 32)
            pieces = [(e, *piece) for e in range(EH) for piece in HPIECES[e]]

            def combine(n):
                e, a, b, _ = pieces[n]
                dve.wait_ge(done["hs"], n + 1)
                if e == 0:
                    ins = dve.tensor_scalar(comb[:, 0, :], hs[:, 0, :], fw[:, 0:1], None, ALU.mult)
                else:
                    dve.wait_ge(done["comb"], e)
                    ins = dve.scalar_tensor_tensor(comb[:, e, a:b], hs[:, e, a:b], fw[:, e:e + 1],
                                                   comb[:, e - 1, a:b], ALU.mult, ALU.add)
                ins.then_inc(done["comb"], 1)

            for n, (e, a, b, psum) in enumerate(pieces):
                dve.wait_ge(done["h_ps"], n + 1)
                dve.tensor_tensor(h[:, e, a:b], bank[psum][:, a:b],
                                  expert_b[:, e * D + a:e * D + b], ALU.add).then_inc(done["h"], 1)
                if n >= 1:
                    combine(n - 1)
            combine(len(pieces) - 1)
            dve.wait_ge(done["y3_ps"], 1)
            dve.tensor_tensor(y[0:T, :], xb[0:T, :], bank[3][0:T, 0:D], ALU.add).then_inc(done["y"], 1)
            dve.wait_ge(done["y"], 1)
            after(dve.tensor_tensor(yn[0:T, :], y[0:T, :], rows_("norm_w"), ALU.mult))
            dve.wait_ge(done["yr"], 1)
            dve.scalar_tensor_tensor(fin[0:T, :], yn[0:T, :], yr[0:T, :], x2[0:T, :],
                                     ALU.mult, ALU.add).then_inc(done["fin"], 1)


def pack(parts, values, rows_=P):
    out = np.zeros((rows_, width(parts)), np.float32)
    for name in parts:
        if name in values:
            a, b = place(parts, name)
            v = values[name]
            out[:v.shape[0], a:a + v.shape[1]] = v
    return out


def by_chunk(w):
    return np.ascontiguousarray(w.reshape(DC, P, -1).transpose(1, 0, 2)).reshape(P, -1)


def rope_tables():
    freq = (1.0 / np.float32(10000.0) ** (np.arange(HALF, dtype=np.float32) / np.float32(HALF))).astype(np.float32)
    ang = (np.arange(LK, dtype=np.float32)[:, None] * freq).astype(np.float32)
    return np.cos(ang).astype(np.float32), np.sin(ang).astype(np.float32)


def kernel(**inputs):
    import concourse.bacc as bacc
    from concourse.bass_utils import run_bass_kernel_spmd

    a = {k: np.asarray(v) for k, v in inputs.items()}
    w = {k[3:]: v for k, v in a.items() if k.startswith("L0_")}
    cos, sin = rope_tables()

    key = np.arange(NG * P) % NKEY
    query = (key // WIN).reshape(NG, P).T
    seg = a["itok_BxS_0_1023"].reshape(T)
    seg_in = np.concatenate([seg[query], np.tile(seg, (P, 1)),
                             ((key % WIN) - LOOKBACK).reshape(NG, P).T,
                             np.tile(np.arange(WIN) + int(SHIFT), (P, 1))], axis=1).astype(seg.dtype)

    c1 = pack(C1, dict(ident=np.eye(P, dtype=np.float32), dq=by_chunk(w["xattn_W_dq"])))
    own = np.arange(P)[:, None] % QPC == np.arange(KPC)[None, :] // WIN
    c2 = pack(C2, dict(
        kvct=w["xattn_W_kvc"].reshape(DC, P, KVC).transpose(0, 2, 1).reshape(P, P),
        kr=np.tile(w["xattn_W_kr"], (DC, 1)), kvc=by_chunk(w["xattn_W_kvc"]),
        block=np.where(own, 0.0, NEG),
        cosq=cos[query].reshape(P, -1), sinq=sin[query].reshape(P, -1),
        headsum=(np.arange(P)[:, None] // DK == np.arange(H)[None, :]),
        twice=np.tile(np.eye(T), (2, 1)), iota=np.tile(np.arange(E), (P, 1))))

    def heads(m, first):
        return m.reshape(first, H, -1)

    uqk = np.concatenate([heads(w["xattn_W_uq"], QC).transpose(2, 1, 0),
                          heads(w["xattn_W_uk"], KVC).transpose(2, 1, 0)], axis=2).reshape(P, -1)
    g = np.concatenate([w[f"attn_{n}"].T.reshape(DC, P, -1)
                        for n in ("Wq", "Wk", "Wkg1", "Wv", "Wg", "Wo")], axis=2)
    kg2 = np.zeros((P, P + 1), np.float32)
    kg2[:GLR, :P] = w["attn_Wkg2"].T
    kg2[:, P] = w["attn_bkg2"]
    arrays = dict(
        seg=seg_in,
        x=a["x"].reshape(T, D),
        c1=c1, c2=c2,
        ctx=np.concatenate([a["ctx_2048"].reshape(LK, D), cos, sin], axis=1),
        uqk=uqk,
        qr=w["xattn_W_qr"],
        uv=heads(w["xattn_W_uv"], KVC).transpose(2, 1, 0).reshape(P, -1),
        wo=w["xattn_W_o"].reshape(H, HD, D).transpose(1, 0, 2).reshape(P, -1),
        gla=g.transpose(1, 0, 2).reshape(P, -1),
        kg2=kg2,
        rows=np.concatenate([w["attn_bg"], w["ffn_proj_b"], w["ffn_norm_w"], w["ffn_router_b"]])[None],
        router=by_chunk(w["ffn_router_w"]),
        expert=w["ffn_expert_w"].reshape(E, DC, P, D).transpose(2, 1, 0, 3).reshape(P, -1),
        expert_b=w["ffn_expert_b"].reshape(2, EH * D),
        proj=by_chunk(w["ffn_proj_w"]))
    arrays = {f"in_{k}": np.ascontiguousarray(v) for k, v in arrays.items()}

    nc = bacc.Bacc("TRN2", target_bir_lowering=False, num_devices=1)
    args = [nc.dram_tensor(k, v.shape, mybir.dt.from_np(v.dtype), kind="ExternalInput").ap()
            for k, v in arrays.items()]
    out = nc.dram_tensor("out", (T, D), F32, kind="ExternalOutput").ap()
    block_kernel(nc, *args, out)
    r = run_bass_kernel_spmd(nc, [arrays], core_ids=[0])
    return r.results[0]["out"].reshape(1, T, D)
```

```python
from contextlib import ExitStack

import numpy as np

import concourse.bass as bass
from concourse import mybir

F32 = mybir.dt.float32
BF16 = mybir.dt.bfloat16
I32 = mybir.dt.int32
U32 = mybir.dt.uint32
ALU = mybir.AluOpType
ACT = mybir.ActivationFunctionType
AX = mybir.AxisListType
RADD = bass.bass_isa.ReduceOp.add

P = 128
T = 64
D = 256
DC = D // P
LK = 6272
H = 16
HP = H // 2
HD = 128
KVC, QC, R = 64, 96, 64
HALF = R // 2
LOOKBACK = 8
WIN = LOOKBACK + 1
NKEY = T * WIN
NG = -(-NKEY // P)
MROW = 7
MTURN = LK // P // MROW
ROW = D + R
QPC = 8
NCH = T // QPC
KPC = QPC * WIN
CTX_PIECES = ((0, 4, 5), (4, 6, 2), (6, 8, 0))
NEG = -1e30
SHIFT = 1000.0
QK_SCALE = float(1.0 / np.sqrt(np.float32(HD + R)))
LN_EPS = 1e-5
DK, DV = 8, 16
HALF_V = DV // 2
Q_PIECES = (0, HALF_V, HALF_V + 4, DV)
GLR = 16
GK_SCALE = 128.0 ** -0.5
GATE_NORM = 16.0
GLA_EPS = 1e-5
E = 8
EH = E // 2
HPIECES = [[(0, D, 6)], [(0, D, 7)], [(0, D, 0)], [(0, P, 1), (P, D, 4)]]
RMS_EPS = 1e-6

SEG = dict(key=NG, row=T, koff=NG, moff=WIN)
C1 = dict(ident=P, dq=DC * QC)
C2 = dict(kvct=P, kr=R, block=KPC, cosq=NG * HALF, sinq=NG * HALF, headsum=H, twice=T, iota=E,
          kvc=DC * KVC)
KEY_PARTS = ((slice(0, 2), 0, 0), (slice(2, 4), 1, 0), (slice(4, NG), 5, 2 * P))
UQK_PARTS = 4
WO_PARTS = 4
GLA = dict(q=P, k=P, kg1=GLR, v=D, g=D, o=D)
ROWS = dict(bg=D, proj_b=D, norm_w=D, router_b=E)


def width(parts):
    return sum(parts.values())


def place(parts, name):
    at = 0
    for n, w in parts.items():
        if n == name:
            return at, at + w
        at += w
    raise KeyError(name)


DUMMIES = dict(xn1=10, xn1t=1, fold=0, wkk=0, fold2=1, kv0=0, fold3=0, kv1=1, q0=0, scores=0, ctx=2, x1h=1, x1t=1, xm2t=1, kg1=0, qstate=12, qstate2=0, og=8, ogt=1, x2t=2, xm3t=2,
               comb=4, combt=0)


def block_kernel(nc, seg_in, x_in, c1_in, c2_in, ctx_in, uqk_in, qr_in, uv_in, wo_in, gla_in,
                 kg2_in, rows_in, router_in, expert_in, expert_b_in, proj_in, out):
    with ExitStack() as ctx:
        def sb(name, cols, dt=F32, rows=P):
            return ctx.enter_context(nc.sbuf_tensor(name, [rows, *cols], dt))

        def sem(name):
            return ctx.enter_context(nc.semaphore(name))

        bank = [ctx.enter_context(nc.psum_tensor(f"bank{i}", [P, 512], F32)) for i in range(8)]

        seg = sb("seg", [width(SEG)], I32)
        x = sb("x", [D])
        xh = sb("xh", [P])
        c1 = sb("c1", [width(C1)])
        c2 = sb("c2", [width(C2) + DC * R])
        keys = sb("keys", [NG, ROW])
        uqk = sb("uqk", [H, QC + KVC])
        aq = sb("aq", [H, KVC])
        qr = sb("qr", [H * R])
        uv = sb("uv", [H, KVC])
        wo = sb("wo", [H, D])
        gla = sb("gla", [DC, width(GLA)])
        kg2 = sb("kg2", [P + 1])
        rows = sb("rows", [width(ROWS)])
        router = sb("router", [DC, E])
        expert = sb("expert", [DC, E, D])
        expert_b = sb("expert_b", [EH * D])
        proj = sb("proj", [DC, D])

        halves = [slice(j * T, (j + 1) * T) for j in range(2)]

        def seg_(name):
            a, b = place(SEG, name)
            return segf[:, a:b]

        def c1_(name):
            a, b = place(C1, name)
            return c1[:, a:b]

        def c2_(name):
            a, b = place(C2, name)
            return c2[:, a:b]

        def gla_(kc, name):
            a, b = place(GLA, name)
            return gla[:, kc, a:b]

        def rows_(name, n=T):
            a, b = place(ROWS, name)
            return rows[0:n, a:b]

        ident = c1_("ident")
        kw = c2[:, width(C2) - DC * KVC:].rearrange("p (s c n) -> p c s n", s=2, c=DC)
        dq = c1_("dq").rearrange("p (c n) -> p c n", c=DC)
        cosq = c2_("cosq").rearrange("p (g r) -> p g r", g=NG)
        sinq = c2_("sinq").rearrange("p (g r) -> p g r", g=NG)

        idle = sb("idle", [512], BF16)
        segf = sb("segf", [width(SEG)])
        segc = sb("segc", [NG + T])
        inside = sb("inside", [NG + T])
        outside = sb("outside", [NG])
        lowest = sb("lowest", [1])
        flag = sb("flag", [1], I32)
        kidx = sb("kidx", [NG])
        kidxu = sb("kidxu", [NG], U32)
        segv = sb("segv", [T])
        pos = sb("pos", [T, WIN])
        posc = sb("posc", [T, WIN])
        maskb = sb("maskb", [NCH, KPC])
        wide = sb("wide", [MROW, D])
        sums = sb("sums", [MROW, D])
        total = sb("total", [D])
        share = sb("share", [D])
        consts = sb("consts", [3])
        eps5, eps6, one = consts[:, 0:1], consts[:, 1:2], consts[:, 2:3]
        stats = sb("stats", [6])
        mv = sb("mv", [2])
        lnv = sb("lnv", [1])
        rstd = sb("rstd", [1])
        xn1 = sb("xn1", [D])
        xn1t = sb("xn1t", [DC * T])
        qct = sb("qct", [T])
        qt = sb("qt", [NCH, H, QPC])
        kt_in = sb("kt_in", [DC, NG * P])
        kr_ = sb("kr_", [NG, 2 * KVC])
        cosr = sb("cosr", [NG, HALF])
        sinr = sb("sinr", [NG, HALF])
        rc = sb("rc", [NG, 2, HALF])
        rs = sb("rs", [NG, 2, HALF])
        ru = sb("ru", [NG, 2, HALF])
        rw = sb("rw", [NG, 2, HALF])
        kt = sb("kt", [NG * P])
        vals = sb("vals", [NCH, KVC])
        s = sb("s", [NCH, KPC])
        nmax = sb("nmax", [NCH])
        p = sb("p", [NCH, KPC])
        psums = sb("psums", [NCH])
        rsum = sb("rsum", [NCH])
        pt = sb("pt", [NCH, P])
        ctxt = sb("ctxt", [HP, T])
        wvo = sb("wvo", [HP, D])
        over_d = sb("over_d", [P])
        x1h = sb("x1h", [P])
        x1t = sb("x1t", [DC, T])

        xm2t = sb("xm2t", [DC, T])
        xsq2 = sb("xsq2", [DC, T])
        lnv2 = sb("lnv2", [T + 1])
        rstd2 = sb("rstd2", [T + 1])
        kg1 = sb("kg1", [T])
        z = sb("z", [T])
        az = sb("az", [T])
        minz = sb("minz", [T])
        ez = sb("ez", [T])
        lz = sb("lz", [T])
        logsig = sb("logsig", [T])
        gates = sb("gates", [DV, T])
        qs = sb("qs", [T])
        ks = sb("ks", [T])
        vrep = sb("vrep", [HALF_V, H, DK])
        kvt = sb("kvt", [DV, T])
        state = sb("state", [DV, T])
        qstate = sb("qstate", [DV, T])
        zg = sb("zg", [D])
        sg = sb("sg", [D])
        wvsum = sb("wvsum", [DC, H])
        wvc = sb("wvc", [DC, H, DV])
        osq = sb("osq", [H, DV])
        ovar = sb("ovar", [H])
        olnv = sb("olnv", [H])
        orstd = sb("orstd", [H])
        ocs = sb("ocs", [H, DV])
        og = sb("og", [H, DV])
        ogt = sb("ogt", [DC * T])
        x2t = sb("x2t", [DC, T])
        x2 = sb("x2", [D])

        xm3t = sb("xm3t", [DC, T])
        xsq3 = sb("xsq3", [DC, T])
        lnv3 = sb("lnv3", [1])
        rstd3 = sb("rstd3", [1])
        xn3 = sb("xn3", [D])
        xb = sb("xb", [D])
        logits = sb("logits", [E])
        top = sb("top", [8])
        topi = sb("topi", [8], U32)
        topf = sb("topf", [8])
        gap = sb("gap", [1])
        tgap = sb("tgap", [1])
        hot1 = sb("hot1", [E])
        hot2 = sb("hot2", [E])
        hsum = sb("hsum", [E])
        hdiff = sb("hdiff", [E])
        fw = sb("fw", [EH])
        h = state[:].rearrange("p (e v) t -> p e (v t)", e=EH)
        hs = kvt[:].rearrange("p (e v) t -> p e (v t)", e=EH)
        comb = qstate[:].rearrange("p (e v) t -> p e (v t)", e=EH)
        combt = sb("combt", [DC * T])
        y = sb("y", [D])
        ysq = sb("ysq", [D])
        yss = sb("yss", [1])
        ylnv = sb("ylnv", [1])
        yr = sb("yr", [1])
        yn = sb("yn", [D])
        fin = sb("fin", [D])

        landed = {n: sem(f"landed_{n}") for n in (
            "seg", "x", "xh", "c1", "c2", "qr", "uv", "gla", "kg2", "rows", "router",
            "expert_b", "proj", "out", "wide")}
        landed_key = [sem(f"landed_key{g}") for g in range(NG)]
        landed_uqk = [sem(f"landed_uqk{i}") for i in range(UQK_PARTS)]
        landed_wo = [sem(f"landed_wo{i}") for i in range(WO_PARTS)]
        landed_expert = [sem(f"landed_expert{i}") for i in range(2)]
        done = {n: sem(f"done_{n}") for n in (
            "consts", "idle", "sums", "kidx", "flag", "keys", "cosr", "maskb",
            "mv1", "rstd1", "xn1", "xn1t_ps", "xn1t", "wkk_ps", "wkk", "qct_ps", "qct",
            "aq_ps", "aq_act", "aq_dve", "kin_ps", "kin", "qt_ps", "qt_act", "qt_dve", "kv_ps",
            "kr_c", "kr_r", "kt_ps", "kt_act", "kt_dve",
            "vals_ps", "vals", "s_ps", "s", "nmax", "s_less_max", "exp", "p", "pt_ps", "pt_dve", "pt_act", "wvo_ps", "wvo",
            "ctx_ps", "ctx_dve", "ctx_act", "y1_ps", "x1h", "x1t_ps", "x1t_act", "x1t_dve", "over_d",
            "mean2_ps", "xm2t", "xsq2", "var2_ps", "rstd2", "kg1_ps", "kg1", "v_ps", "v_act",
            "v_dve", "qk_ps", "qs", "ks", "kg_ps", "z", "az", "minz", "lz", "logsig", "gates_start",
            "gates", "g_ps", "zg", "sg",
            "wvc", "vrep_ps", "kvt", "state", "qstate", "o_ps", "osq", "ovar", "orstd",
            "og", "ogt_ps", "ogt_act", "ogt_dve", "y2_ps", "x2t",
            "mean3_ps", "xm3t", "xsq3", "var3_ps", "rstd3", "x2_ps", "xn3", "xb", "lg_ps", "gap", "topf", "hot", "hotpm", "fw",
            "tgap", "h_ps", "h",
            "hs", "comb", "combt_ps", "combt", "y3_ps", "y", "yss", "yr", "fin")}
        mean_step = sem("mean_step")
        act_step = sem("act_step")
        dve_step = sem("dve_step")

        def stepper(eng, step_sem):
            count = [0]

            def after(ins):
                count[0] += 1
                ins.then_inc(step_sem, 1)
                eng.wait_ge(step_sem, count[0])
            return after

        block = ctx.enter_context(nc.Block())

        @block.sync
        def _(sp):
            def load(dst, src, signal):
                sp.dma_start(dst, src).then_inc(signal, 16)

            load(seg[:], seg_in, landed["seg"])
            load(c1[:], c1_in, landed["c1"])

            def load_uqk(i):
                n = H * (QC + KVC) // UQK_PARTS
                load(uqk[:].rearrange("p h n -> p (h n)")[:, i * n:(i + 1) * n],
                     uqk_in[:, i * n:(i + 1) * n], landed_uqk[i])

            load_uqk(0)
            load_uqk(1)
            load(c2[:, 0:width(C2)], c2_in, landed["c2"])
            sp.wait_ge(landed_uqk[0], 16)
            load_uqk(2)
            sp.wait_ge(landed_uqk[1], 16)
            load_uqk(3)
            sp.wait_ge(landed_uqk[2], 16)
            load(qr[0:QC, :], qr_in, landed["qr"])
            sp.wait_ge(landed_uqk[3], 16)
            load(uv[:].rearrange("p h n -> p (h n)"), uv_in, landed["uv"])
            n = H * D // WO_PARTS
            for i in range(WO_PARTS):
                load(wo[:].rearrange("p h n -> p (h n)")[:, i * n:(i + 1) * n],
                     wo_in[:, i * n:(i + 1) * n], landed_wo[i])
            load(gla[:].rearrange("p c n -> p (c n)"), gla_in, landed["gla"])
            load(kg2[:], kg2_in, landed["kg2"])
            load(rows[:], rows_in.broadcast_to([P, width(ROWS)]), landed["rows"])
            for j in range(2):
                load(xh[halves[j], :], x_in[:, j * P:(j + 1) * P], landed["xh"])
            load(router[:].rearrange("p c n -> p (c n)"), router_in, landed["router"])
            for g in range(2):
                load(expert_b[g * T:(g + 1) * T, :],
                     expert_b_in[g:g + 1, :].broadcast_to([T, EH * D]), landed["expert_b"])
            for kc in range(DC):
                load(expert[:, kc].rearrange("p e n -> p (e n)"),
                     expert_in[:, kc * E * D:(kc + 1) * E * D], landed_expert[kc])
            load(proj[:].rearrange("p c n -> p (c n)"), proj_in, landed["proj"])
            sp.wait_ge(done["fin"], 1)
            sp.dma_start(out, fin[0:T, :]).then_inc(landed["out"], 16)
            sp.wait_ge(landed["out"], 16)

        @block.gpsimd
        def _(pool):
            pool.wait_ge(done["kidx"], 1)
            for g in range(NG):
                pool.indirect_dma_start(
                    out=keys[:, g, :], out_offset=None, in_=ctx_in,
                    in_offset=bass.IndirectOffsetOnAxis(ap=kidxu[:, g:g + 1], axis=0),
                ).then_inc(landed_key[g], 16)
            pool.wait_ge(done["flag"], 1)
            some_outside = nc.values_load(flag[0:1, 0:1], engines=[mybir.EngineType.Pool],
                                          min_val=0, max_val=1)
            with pool.If(some_outside > 0):
                mean_after = stepper(pool, mean_step)
                mean_after(pool.memset(sums[:], 0.0))
                rows_by_turn = ctx_in.rearrange("(p n) d -> p n d", p=P)
                with pool.Fori(0, MTURN) as turn:
                    pool.dma_start(wide[:], rows_by_turn[:, bass.ds(turn * MROW, MROW), 0:D]
                                   ).then_inc(landed["wide"], 16)
                    pool.wait_ge(landed["wide"], turn * 16 + 16)
                    pool.tensor_tensor(sums[:], sums[:], wide[:], ALU.add).then_inc(done["sums"], 1)
                    pool.wait_ge(done["sums"], turn + 1)
                for n in range(1, MROW):
                    mean_after(pool.tensor_tensor(sums[:, 0], sums[:, 0], sums[:, n], ALU.add))
                mean_after(pool.partition_all_reduce(total[:], sums[:, 0], P, RADD))
                for g in range(NG):
                    pool.wait_ge(landed_key[g], 16)
                    mean_after(pool.tensor_scalar(share[:], total[:], outside[:, g:g + 1], 1.0 / LK,
                                             ALU.mult, ALU.mult))
                    mean_after(pool.tensor_scalar(keys[:, g, 0:D], keys[:, g, 0:D],
                                             inside[:, g:g + 1], None, ALU.mult))
                    mean_after(pool.tensor_tensor(keys[:, g, 0:D], keys[:, g, 0:D], share[:], ALU.add))
            pool.end_ifs()
            pool.memset(share[:, 0:1], 0.0).then_inc(done["keys"], 1)
            pool.wait_ge(done["topf"], 1)
            pool.wait_ge(landed["c2"], 16)
            pool.tensor_scalar(hot1[:], c2_("iota"), topf[:, 0:1], 0.5, ALU.is_equal,
                               ALU.mult).then_inc(done["hot"], 1)
            pool.tensor_scalar(hot2[:], c2_("iota"), topf[:, 1:2], 0.5, ALU.is_equal,
                               ALU.mult).then_inc(done["hot"], 1)
            pool.wait_ge(done["hot"], 2)
            pool.tensor_tensor(hsum[:], hot1[:], hot2[:], ALU.add).then_inc(done["hotpm"], 1)
            pool.tensor_tensor(hdiff[:], hot1[:], hot2[:], ALU.subtract).then_inc(done["hotpm"], 1)
            pool.wait_ge(landed["rows"], 16)
            pool.wait_ge(done["xn3"], 1)
            pool.tensor_tensor(xb[0:T, :], xn3[0:T, :], rows_("proj_b"), ALU.add).then_inc(
                done["xb"], 1)

        def kv_psum(i):
            part, b, at = KEY_PARTS[i]
            n = part.stop - part.start
            return bank[b][:, at:at + n * P].rearrange("p (g s c) -> p g s c", s=2, c=KVC)

        def attended(copy, eng, i):
            first, end, b = CTX_PIECES[i]
            eng.wait_ge(done["ctx_ps"], i + 1)
            return copy(ctxt[:, :, first * QPC:end * QPC],
                        bank[b][:, 0:HP * (end - first) * QPC].rearrange("p (h t) -> p h t", h=HP))

        def value_columns(b):
            v = bank[b][:, 0:4 * H].rearrange("t (h v) -> t v h", v=4)
            return v.unsqueeze(3).broadcast_to([P, 4, H, DK])

        @block.scalar
        def _(act):
            after = stepper(act, act_step)
            act.dma_start(x[0:T, :], x_in).then_inc(landed["x"], 16)
            act.preload_act_table_set("natural_log_exp_and_others")
            act.wait_ge(done["consts"], 3)

            act.wait_ge(done["mv1"], 1)
            after(act.activation(lnv[0:T, :], mv[0:T, 1:2], ACT.Ln, bias=eps5[0:T, :]))
            act.activation(rstd[0:T, :], lnv[0:T, :], ACT.Exp, scale=-0.5).then_inc(
                done["rstd1"], 1)
            act.wait_ge(done["xn1t_ps"], 1)
            act.copy(xn1t[:], bank[0][:, 0:P]).then_inc(done["xn1t"], 1)
            act.wait_ge(done["qct_ps"], 1)
            act.copy(qct[0:QC, :], bank[0][0:QC, P:P + T]).then_inc(done["qct"], 1)
            act.wait_ge(done["aq_ps"], 1)
            act.copy(aq[0:QC, 0:HP, :], bank[1][0:QC, :].rearrange("p (h c) -> p h c", c=KVC)).then_inc(
                done["aq_act"], 1)

            def rows_transposed(i):
                part = KEY_PARTS[i][0]
                n = part.stop - part.start
                act.wait_ge(done["kin_ps"], i + 1)
                act.copy(kt_in[:, :, part.start * P:part.stop * P].rearrange(
                             "p c (g k) -> p g c k", g=n),
                         bank[3 + i][:, 0:n * D].rearrange("p (g c k) -> p g c k", g=n,
                                                          c=DC)).then_inc(done["kin"], 1)

            def kv_c_by_key(i):
                act.wait_ge(done["kv_ps"], i + 1)
                act.copy(kr_[:, KEY_PARTS[i][0], 0:KVC], kv_psum(i)[:, :, 0, :]).then_inc(
                    done["kr_c"], 1)

            rows_transposed(0)
            kv_c_by_key(0)
            rows_transposed(1)
            kv_c_by_key(1)
            rows_transposed(2)
            act.wait_ge(done["qt_ps"], 1)
            act.copy(qt[:, :, 0:HP, :].rearrange("p c h q -> p h c q"),
                     bank[6][:].rearrange("p (h c q) -> p h c q", h=HP, q=QPC)).then_inc(
                done["qt_act"], 1)
            kv_c_by_key(2)
            act.wait_ge(done["kt_ps"], 1)
            act.copy(kt[:, 0:256], bank[3][:, 0:256]).then_inc(done["kt_act"], 1)
            act.wait_ge(done["kt_ps"], 3)
            act.copy(kt[:, 512:640], bank[0][:, 0:P]).then_inc(done["kt_act"], 1)

            def folded_uv(i):
                act.wait_ge(done["wvo_ps"], i + 1)
                act.copy(wvo[:, 2 * i:2 * i + 2, :].rearrange("p h n -> p (h n)"),
                         bank[(6, 7, 0, 4)[i]][:]).then_inc(done["wvo"], 1)

            folded_uv(0)
            for c in range(NCH // 2):
                act.wait_ge(done["nmax"], 1)
                act.activation(p[:, c, :], s[:, c, :], ACT.Exp, bias=nmax[:, c:c + 1],
                               accum_out=psums[:, c:c + 1]).then_inc(done["exp"], 1)
            act.wait_ge(done["s_less_max"], 1)
            act.activation(p[:, NCH // 2:, :], s[:, NCH // 2:, :], ACT.Exp).then_inc(done["exp"], 1)
            act.wait_ge(done["vals_ps"], 1)
            act.copy(vals[0:KPC], bank[5][0:KPC, :].rearrange("p (c v) -> p c v", v=KVC)).then_inc(
                done["vals"], 1)
            for i in range(1, 4):
                folded_uv(i)
            act.wait_ge(done["pt_ps"], 2)
            act.copy(pt[0:KPC, 4:, :].rearrange("k c n -> k (c n)"), bank[1][0:KPC, :]).then_inc(
                done["pt_act"], 1)
            attended(act.copy, act, 2).then_inc(done["ctx_act"], 1)
            act.wait_ge(done["x1t_ps"], 1)
            act.copy(x1t[:, 0, :], bank[3][:, 0:T]).then_inc(done["x1t_act"], 1)

            act.wait_ge(done["xm2t"], 1)
            act.activation(xsq2[:], xm2t[:], ACT.Square).then_inc(done["xsq2"], 1)
            act.wait_ge(done["var2_ps"], 1)
            after(act.activation(lnv2[:, 0:T], bank[0][:, 0:T], ACT.Ln, bias=eps5))
            act.activation(rstd2[:, 0:T], lnv2[:, 0:T], ACT.Exp, scale=-0.5).then_inc(
                done["rstd2"], 1)
            act.wait_ge(done["var2_ps"], 2)
            after(act.activation(lnv2[:, T:], bank[4][:, 0:1], ACT.Ln, bias=eps5))
            act.activation(rstd2[:, T:], lnv2[:, T:], ACT.Exp, scale=-0.5).then_inc(
                done["rstd2"], 1)
            act.wait_ge(landed["kg2"], 16)
            act.wait_ge(done["z"], 1)
            act.activation(az[:], z[:], ACT.Abs, bias=kg2[:, P:P + 1]).then_inc(
                done["az"], 1)
            act.wait_ge(done["az"], 1)
            after(act.activation(ez[:], az[:], ACT.Exp, scale=-1.0))
            act.activation(lz[:], ez[:], ACT.Ln, bias=one).then_inc(done["lz"], 1)
            act.wait_ge(done["rstd2"], 2)
            act.wait_ge(done["v_ps"], 1)
            act.mul(vrep[:, 0:4], value_columns(2), rstd2[:, T:T + 1]).then_inc(done["v_act"], 1)
            act.wait_ge(done["logsig"], 1)
            for j in range(2):
                act.activation(gates[:, 8 * j:8 * j + 8, 1:T],
                               logsig[:, 1:T].unsqueeze(1).broadcast_to([P, 8, T - 1]), ACT.Exp,
                               scale=1.0 / GATE_NORM).then_inc(done["gates"], 1)
            act.preload_act_table(ACT.Silu)
            act.wait_ge(done["zg"], 1)
            act.activation(sg[0:T, :], zg[0:T, :], ACT.Silu).then_inc(done["sg"], 1)
            act.preload_act_table_set("natural_log_exp_and_others")
            act.wait_ge(done["o_ps"], 1)
            act.activation(osq[0:T], bank[1][0:T, 0:D].rearrange("p (v h) -> p h v", h=H),
                           ACT.Square).then_inc(done["osq"], 1)
            act.wait_ge(done["ovar"], 1)
            after(act.activation(olnv[0:T, :], ovar[0:T, :], ACT.Ln, bias=eps5[0:T, :],
                                 scale=1.0 / DV))
            act.activation(orstd[0:T, :], olnv[0:T, :], ACT.Exp, scale=-0.5).then_inc(done["orstd"], 1)
            act.wait_ge(done["ogt_ps"], 1)
            act.copy(ogt[:, 0:T], bank[2][:, 0:T]).then_inc(done["ogt_act"], 1)

            act.wait_ge(done["xm3t"], 1)
            act.activation(xsq3[:], xm3t[:], ACT.Square).then_inc(done["xsq3"], 1)
            act.wait_ge(done["var3_ps"], 1)
            after(act.activation(lnv3[:], bank[4][:, 0:1], ACT.Ln, bias=eps5))
            act.activation(rstd3[:], lnv3[:], ACT.Exp, scale=-0.5).then_inc(done["rstd3"], 1)
            act.preload_act_table(ACT.Silu)
            act.wait_ge(done["gap"], 1)
            act.activation(tgap[:], gap[:], ACT.Tanh, scale=0.5).then_inc(done["tgap"], 1)
            n = 0
            for e in range(EH):
                for a, b, _ in HPIECES[e]:
                    n += 1
                    act.wait_ge(done["h"], n)
                    act.activation(hs[:, e, a:b], h[:, e, a:b], ACT.Silu).then_inc(done["hs"], 1)
            act.wait_ge(done["x2_ps"], 1)
            act.wait_ge(done["rstd3"], 1)
            act.mul(xn3[0:T, :], bank[2][0:T, D:], rstd3[0:T, :]).then_inc(done["xn3"], 1)
            act.copy(x2[0:T, :], bank[2][0:T, 0:D])
            act.preload_act_table_set("natural_log_exp_and_others")
            act.wait_ge(done["y"], 1)
            after(act.activation(ysq[0:T, :], y[0:T, :], ACT.Square, accum_out=yss[0:T, :]))
            after(act.activation(ylnv[0:T, :], yss[0:T, :], ACT.Ln, bias=eps6[0:T, :],
                                 scale=1.0 / D))
            act.activation(yr[0:T, :], ylnv[0:T, :], ACT.Exp, scale=-0.5).then_inc(done["yr"], 1)

        @block.tensor
        def _(pe):
            def transpose_tokens(src, psum, signal):
                for kc in range(DC):
                    mm = pe.transpose(psum[:, kc * T:(kc + 1) * T],
                                      src[0:T, kc * P:(kc + 1) * P], ident[0:T, 0:T])
                mm.then_inc(signal, 1)

            def keep_clock(before, psum):
                for _ in range(DUMMIES[before]):
                    pe.matmul(psum[:], idle[:, 0:P], idle[:], start=True, stop=True)

            pe.wait_ge(done["idle"], 1)
            keep_clock("xn1", bank[7])
            pe.wait_ge(landed["c1"], 16)
            pe.wait_ge(done["xn1"], 1)
            transpose_tokens(xn1, bank[0], done["xn1t_ps"])
            keep_clock("xn1t", bank[7])
            pe.wait_ge(done["xn1t"], 1)
            for kc in range(DC):
                mm = pe.matmul(bank[0][0:QC, P:P + T], dq[:, kc, :],
                               xn1t[:, kc * T:(kc + 1) * T], start=kc == 0, stop=kc == DC - 1)
            mm.then_inc(done["qct_ps"], 1)

            def fold_uk(i):
                pe.wait_ge(landed_uqk[i], 16)
                n = H // UQK_PARTS
                for hh in range(n * i, n * (i + 1)):
                    mm = pe.matmul(bank[1 + hh // HP][0:QC, hh % HP * KVC:(hh % HP + 1) * KVC],
                                   uqk[:, hh, 0:QC], uqk[:, hh, QC:], start=True, stop=True)
                if i % 2 == 1:
                    mm.then_inc(done["aq_ps"], 1)

            def transpose_keys(g):
                pe.wait_ge(landed_key[g], 16)
                for kc in range(DC):
                    at = g % 2 * D + kc * P
                    mm = pe.transpose(bank[3 + g // 2][:, at:at + P],
                                      keys[:, g, kc * P:(kc + 1) * P], ident)
                if g % 2 == 1 or g == NG - 1:
                    mm.then_inc(done["kin_ps"], 1)

            def project_keys(i):
                part, b, at = KEY_PARTS[i]
                pe.wait_ge(done["kin"], i + 1)
                for g in range(part.start, part.stop):
                    for kc in range(DC):
                        mm = pe.matmul(bank[b][:, at + g % 2 * P:at + (g % 2 + 1) * P],
                                       kt_in[:, kc, g * P:(g + 1) * P], kw[:, kc],
                                       start=kc == 0, stop=kc == DC - 1)
                mm.then_inc(done["kv_ps"], 1)

            def queries(first):
                for hh in range(first, first + HP):
                    cols = slice(hh % HP * T, (hh % HP + 1) * T)
                    pe.matmul(bank[6 + hh // HP][KVC:P, cols],
                              qr[0:QC, hh * R:(hh + 1) * R], qct[0:QC, :], start=True, stop=True)
                    mm = pe.matmul(bank[6 + hh // HP][0:KVC, cols],
                                   aq[0:QC, hh, :], qct[0:QC, :], start=True, stop=True)
                mm.then_inc(done["qt_ps"], 1)

            def transpose_kr(i, b):
                part = KEY_PARTS[i][0]
                pe.wait_ge(done["kr_c"], i + 1)
                pe.wait_ge(done["kr_r"], 2 * (i + 1))
                for g in range(part.start, part.stop):
                    mm = pe.transpose(bank[b][:, g % 2 * P:(g % 2 + 1) * P], kr_[:, g, :], ident)
                mm.then_inc(done["kt_ps"], 1)

            def fold_uv(i):
                pe.wait_ge(landed_wo[i], 16)
                for hh in range(4 * i, 4 * i + 4):
                    half, at = hh % 2 * KVC, hh // 2 % 2 * D
                    mm = pe.matmul(bank[(6, 7, 0, 4)[i]][half:half + KVC, at:at + D],
                                   uv[:, hh, :], wo[:, hh, :], start=True, stop=True)
                mm.then_inc(done["wvo_ps"], 1)

            keep_clock("fold", bank[7])
            fold_uk(0)
            fold_uk(1)
            keep_clock("wkk", bank[7])
            pe.wait_ge(landed["c2"], 16)
            pe.wait_ge(done["qct"], 1)
            for kc in range(DC):
                half = slice(kc * KVC, (kc + 1) * KVC)
                pe.matmul(bank[5 * kc][:, 256:256 + R], c2_("kvct")[half, :], c2_("kr")[half, :],
                          start=True, stop=True).then_inc(done["wkk_ps"], 1)
            pe.wait_ge(done["keys"], 1)
            transpose_keys(0)
            transpose_keys(1)
            keep_clock("fold2", bank[7])
            fold_uk(2)
            keep_clock("kv0", bank[7])
            pe.wait_ge(done["wkk"], 2)
            project_keys(0)
            transpose_keys(2)
            transpose_keys(3)
            keep_clock("fold3", bank[7])
            fold_uk(3)
            keep_clock("kv1", bank[7])
            pe.wait_ge(done["aq_act"], 1)
            project_keys(1)
            transpose_keys(4)
            keep_clock("q0", bank[7])
            pe.wait_ge(landed["qr"], 16)
            queries(0)
            project_keys(2)
            transpose_kr(0, 3)
            transpose_kr(1, 4)
            pe.wait_ge(done["aq_dve"], 1)
            queries(HP)
            transpose_kr(2, 0)
            pe.wait_ge(landed["uv"], 16)
            pe.wait_ge(done["qt_act"], 1)
            fold_uv(0)
            keep_clock("scores", bank[2])
            pe.wait_ge(done["qt_act"], 1)
            pe.wait_ge(done["qt_dve"], 1)
            for c in range(NCH):
                if c == 0:
                    pe.wait_ge(done["kt_act"], 1)
                elif c == 2 * P // KPC:
                    pe.wait_ge(done["kt_dve"], 1)
                elif c == 4 * P // KPC:
                    pe.wait_ge(done["kt_act"], 2)
                mm = pe.matmul(bank[1 + c // 4][:, c % 4 * KPC:(c % 4 + 1) * KPC],
                               qt[:, c].rearrange("p h q -> p (h q)"), kt[:, c * KPC:(c + 1) * KPC],
                               start=True, stop=True)
                if c % 4 == 3:
                    mm.then_inc(done["s_ps"], 1)
            for c in range(NCH):
                mm = pe.transpose(bank[5][0:KPC, c * KVC:(c + 1) * KVC],
                                  kt[0:KVC, c * KPC:(c + 1) * KPC], ident[0:KVC, 0:KVC])
            mm.then_inc(done["vals_ps"], 1)
            def transpose_probs(j):
                pe.wait_ge(done["p"], j + 1)
                for c in range(4 * j, 4 * j + 4):
                    mm = pe.transpose(bank[(3, 1)[j]][0:KPC, c % 4 * P:(c % 4 + 1) * P], p[:, c, :],
                                      ident)
                mm.then_inc(done["pt_ps"], 1)

            for i in range(1, 3):
                fold_uv(i)
            transpose_probs(0)
            fold_uv(3)
            transpose_probs(1)
            pe.wait_ge(done["vals"], 1)
            for first, end, b in CTX_PIECES:
                if first == 0:
                    pe.wait_ge(done["pt_dve"], 1)
                elif first == 4:
                    pe.wait_ge(done["pt_act"], 1)
                elif b == 0:
                    pe.wait_ge(done["wvo"], 3)
                n = (end - first) * QPC
                for c in range(first, end):
                    probs = pt[0:KPC, c, :].rearrange("k (h e q) -> k h e q", e=2, q=QPC)
                    at = (c - first) * QPC
                    for half in range(2):
                        dst = bank[b][half * KVC:(half + 1) * KVC, 0:HP * n]
                        mm = pe.matmul(dst.rearrange("v (h t) -> v h t", h=HP)[:, :, at:at + QPC],
                                       vals[0:KPC, c, :], probs[:, :, half, :], start=True, stop=True)
                mm.then_inc(done["ctx_ps"], 1)
            pe.wait_ge(done["wvo"], 4)
            keep_clock("ctx", bank[7])
            pe.wait_ge(done["ctx_dve"], 2)
            pe.wait_ge(done["ctx_act"], 1)
            for j in range(2):
                for hp in range(HP):
                    mm = pe.matmul(bank[6][halves[j], 0:P], ctxt[:, hp, :],
                                   wvo[:, hp, j * P:(j + 1) * P], start=hp == 0, stop=hp == HP - 1)
            mm.then_inc(done["y1_ps"], 1)

            def transpose_halves(banks, src, signal):
                for j in range(2):
                    pe.transpose(bank[banks[j]][:, 0:T], src[halves[j], :],
                                 ident[halves[j], halves[j]]).then_inc(signal, 1)

            keep_clock("x1h", bank[7])
            pe.wait_ge(done["x1h"], 1)
            transpose_halves((3, 1), x1h, done["x1t_ps"])

            def mean_of(psum, src, signal):
                for kc in range(DC):
                    mm = pe.matmul(psum[:, 0:T], over_d[:], src[:, kc, :],
                                   start=kc == 0, stop=kc == DC - 1)
                mm.then_inc(signal, 1)

            def mean_by_token(psum, src):
                for half in range(2):
                    for kc in range(DC):
                        mm = pe.matmul(psum[half * T:(half + 1) * T, :], src[:, kc, :],
                                       over_d[:, 0:1], start=kc == 0, stop=kc == DC - 1)
                return mm

            keep_clock("x1t", bank[7])
            pe.wait_ge(done["over_d"], 1)
            pe.wait_ge(done["x1t_act"], 1)
            pe.wait_ge(done["x1t_dve"], 1)
            mean_of(bank[4], x1t, done["mean2_ps"])
            keep_clock("xm2t", bank[7])
            pe.wait_ge(done["xm2t"], 1)
            pe.wait_ge(landed["gla"], 16)

            def x_by_feature(psum, name):
                for kc in range(DC):
                    mm = pe.matmul(psum, gla_(kc, name), xm2t[:, kc, :],
                                   start=kc == 0, stop=kc == DC - 1)
                return mm

            x_by_feature(bank[1][0:GLR, 0:T], "kg1").then_inc(done["kg1_ps"], 1)
            pe.wait_ge(done["wvc"], 2)

            keep_clock("kg1", bank[7])
            pe.wait_ge(done["xsq2"], 1)
            for kc in range(DC):
                mm = pe.matmul(bank[0][:, 0:T], over_d[:], xsq2[:, kc, :],
                               start=kc == 0, stop=kc == DC - 1)
            mm.then_inc(done["var2_ps"], 1)
            pe.wait_ge(done["kg1"], 1)
            pe.wait_ge(landed["kg2"], 16)
            pe.matmul(bank[7][:, 0:T], kg2[0:GLR, 0:P], kg1[0:GLR, :], start=True,
                      stop=True).then_inc(done["kg_ps"], 1)
            mean_by_token(bank[4][:, 0:1], xsq2).then_inc(done["var2_ps"], 1)
            for i in range(2):
                for j in range(2):
                    for kc in range(DC):
                        v = HALF_V * j + 4 * i
                        mm = pe.matmul(bank[2 + i][halves[j], 0:4 * H], xm2t[:, kc, :],
                                       wvc[:, kc, :, v:v + 4], start=kc == 0, stop=kc == DC - 1)
                mm.then_inc(done["v_ps"], 1)
            x_by_feature(bank[5][:, 0:T], "q")
            x_by_feature(bank[5][:, T:2 * T], "k").then_inc(done["qk_ps"], 1)
            for v in (4, 5, 6, 7, 0, 1, 2, 3):
                if v % 4 == 0:
                    pe.wait_ge(done["v_dve" if v == 4 else "v_act"], 1)
                for j in range(2):
                    mm = pe.transpose(bank[6 + j][:, v * T:(v + 1) * T],
                                      vrep[halves[j], v].rearrange("p h k -> p (h k)"),
                                      ident[halves[j], halves[j]])
            mm.then_inc(done["vrep_ps"], 1)
            pe.wait_ge(done["rstd2"], 2)
            for kc in range(DC):
                mm = pe.matmul(bank[4][0:T, 0:D], xm2t[:, kc, :], gla_(kc, "g"),
                               start=kc == 0, stop=kc == DC - 1)
            mm.then_inc(done["g_ps"], 1)
            pe.wait_ge(done["qs"], 1)
            keep_clock("qstate", bank[5])
            for v in range(DV):
                if v in Q_PIECES:
                    if v == HALF_V:
                        keep_clock("qstate2", bank[5])
                    pe.wait_ge(done["qstate"], Q_PIECES.index(v) + 1)
                mm = pe.matmul(bank[1][0:T, v * H:(v + 1) * H], qstate[:, v, :], c2_("headsum"),
                               start=True, stop=True)
            mm.then_inc(done["o_ps"], 1)
            keep_clock("og", bank[5])
            for kc in range(DC):
                pe.wait_ge(done["og"], kc + 1)
                pe.transpose(bank[(2, 0)[kc]][:, 0:T],
                             og[0:T].rearrange("p h v -> p (h v)")[:, kc * P:(kc + 1) * P],
                             ident[0:T, 0:T]).then_inc(done["ogt_ps"], 1)
            keep_clock("ogt", bank[5])
            pe.wait_ge(done["ogt_act"], 1)
            pe.wait_ge(done["ogt_dve"], 1)
            for n in range(DC):
                for kc in range(DC):
                    mm = pe.matmul(bank[3][:, n * T:(n + 1) * T],
                                   gla_(kc, "o")[:, n * P:(n + 1) * P],
                                   ogt[:, kc * T:(kc + 1) * T],
                                   start=kc == 0, stop=kc == DC - 1)
            mm.then_inc(done["y2_ps"], 1)

            keep_clock("x2t", bank[5])
            pe.wait_ge(done["x2t"], 1)
            mean_of(bank[2], x2t, done["mean3_ps"])
            keep_clock("xm3t", bank[5])
            pe.wait_ge(done["xm3t"], 1)
            pe.wait_ge(landed["router"], 16)
            for half in range(2):
                for kc in range(DC):
                    mm = pe.matmul(bank[5][half * T:(half + 1) * T, 0:E],
                                   xm3t[:, kc, :], router[:, kc, :],
                                   start=kc == 0, stop=kc == DC - 1)
            mm.then_inc(done["lg_ps"], 1)
            pe.wait_ge(done["xsq3"], 1)
            mean_by_token(bank[4][:, 0:1], xsq3).then_inc(done["var3_ps"], 1)
            for kc in range(DC):
                pe.wait_ge(landed_expert[kc], 16)
            for e in range(EH):
                for a, b, psum in HPIECES[e]:
                    if psum == 4:
                        pe.wait_ge(done["rstd3"], 1)
                    for half in range(2):
                        for kc in range(DC):
                            mm = pe.matmul(bank[psum][half * T:(half + 1) * T, a:b],
                                           xm3t[:, kc, :],
                                           expert[:, kc, half * EH + e, a:b],
                                           start=kc == 0, stop=kc == DC - 1)
                    mm.then_inc(done["h_ps"], 1)
            for i, src in enumerate((x2t, xm3t)):
                for kc in range(DC):
                    at = i * D + kc * P
                    mm = pe.transpose(bank[2][0:T, at:at + P], src[:, kc, :], ident)
            mm.then_inc(done["x2_ps"], 1)
            keep_clock("comb", bank[3])
            for kc in range(DC):
                pe.wait_ge(done["comb"], EH + kc)
                pe.matmul(bank[(5, 0)[kc]][:, 0:T], comb[:, EH - 1, kc * P:(kc + 1) * P],
                          c2_("twice"), start=True, stop=True).then_inc(done["combt_ps"], 1)
            keep_clock("combt", bank[3])
            pe.wait_ge(landed["proj"], 16)
            for kc in range(DC):
                pe.wait_ge(done["combt"], kc + 1)
                mm = pe.matmul(bank[3][0:T, 0:D], combt[:, kc * T:(kc + 1) * T], proj[:, kc, :],
                               start=kc == 0, stop=kc == DC - 1)
            mm.then_inc(done["y3_ps"], 1)

        @block.vector
        def _(dve):
            after = stepper(dve, dve_step)

            dve.memset(eps5, LN_EPS).then_inc(done["consts"], 1)
            dve.memset(eps6, RMS_EPS).then_inc(done["consts"], 1)
            dve.memset(one, 1.0).then_inc(done["consts"], 1)
            dve.memset(idle[:], 0.0).then_inc(done["idle"], 1)
            dve.memset(over_d[:], 1.0 / D).then_inc(done["over_d"], 1)

            def spread(per_chunk):
                return per_chunk.unsqueeze(2).broadcast_to([P, NCH // 2, KPC])

            dve.wait_ge(landed["seg"], 16)
            after(dve.tensor_copy(segf[:], seg[:]))
            after(dve.tensor_tensor(kidx[:], seg_("key"), seg_("koff"), ALU.add))
            dve.tensor_scalar(kidxu[:], kidx[:], 0.0, float(LK - 1), ALU.max, ALU.min).then_inc(
                done["kidx"], 1)
            dve.wait_ge(landed["x"], 16)
            after(dve.bn_stats(stats[0:T, :], x[0:T, :]))
            dve.bn_aggr(mv[0:T, :], stats[0:T, :]).then_inc(done["mv1"], 1)
            after(dve.tensor_scalar(segc[:], segf[:, 0:NG + T], 0.0, float(LK - 1 + LOOKBACK), ALU.max,
                                    ALU.min))
            after(dve.tensor_tensor(inside[:], segc[:], segf[:, 0:NG + T], ALU.is_equal))
            after(dve.tensor_scalar(outside[:], inside[:, 0:NG], -1.0, 1.0, ALU.mult, ALU.add))
            after(dve.tensor_reduce(lowest[:], inside[:, NG:], AX.X, ALU.min))
            dve.tensor_scalar(flag[:], lowest[:], -1.0, 1.0, ALU.mult, ALU.add).then_inc(
                done["flag"], 1)
            dve.wait_ge(done["mv1"], 1)
            dve.wait_ge(done["rstd1"], 1)
            dve.tensor_scalar(xn1[0:T, :], x[0:T, :], mv[0:T, 0:1], rstd[0:T, :],
                              ALU.subtract, ALU.mult).then_inc(done["xn1"], 1)
            after(dve.scalar_tensor_tensor(segv[:], segc[:, NG:], -SHIFT, inside[:, NG:], ALU.add,
                                           ALU.mult))
            after(dve.tensor_tensor(pos[:], segv[:].unsqueeze(2).broadcast_to([P, T, WIN]),
                                    seg_("moff").unsqueeze(1).broadcast_to([P, T, WIN]), ALU.add))
            after(dve.tensor_scalar(posc[:], pos[:], float(LOOKBACK), float(LK - 1 + LOOKBACK),
                                    ALU.max, ALU.min))
            after(dve.tensor_tensor(pos[:], pos[:], posc[:], ALU.not_equal))
            dve.memset(gates[:, :, 0:1], 0.0).then_inc(done["gates_start"], 1)
            for kc in range(DC):
                dve.wait_ge(done["wkk_ps"], kc + 1)
                dve.tensor_copy(kw[:, kc, 1, :], bank[5 * kc][:, 256:256 + R]).then_inc(
                    done["wkk"], 1)
            dve.scalar_tensor_tensor(
                maskb[:], pos[:].rearrange("p (c q) m -> p c (q m)", c=NCH), NEG,
                c2_("block").unsqueeze(1).broadcast_to([P, NCH, KPC]), ALU.mult, ALU.add,
            ).then_inc(done["maskb"], 1)
            def relative(i):
                part = KEY_PARTS[i][0]
                n = part.stop - part.start
                for g in range(part.start, part.stop):
                    dve.wait_ge(landed_key[g], 16)
                both = keys[:, part, D:D + R].rearrange("p g (s r) -> p g s r", s=2)
                dve.tensor_tensor(rc[:, part], both,
                                  cosq[:, part].unsqueeze(2).broadcast_to([P, n, 2, HALF]), ALU.mult)
                after(dve.tensor_tensor(rs[:, part], both,
                                        sinq[:, part].unsqueeze(2).broadcast_to([P, n, 2, HALF]),
                                        ALU.mult))
                dve.tensor_tensor(cosr[:, part], rc[:, part, 0, :], rs[:, part, 1, :],
                                  ALU.add).then_inc(done["cosr"], 1)
                dve.tensor_tensor(sinr[:, part], rc[:, part, 1, :], rs[:, part, 0, :],
                                  ALU.subtract).then_inc(done["cosr"], 1)

            def rotate(i):
                part = KEY_PARTS[i][0]
                n = part.stop - part.start
                dve.wait_ge(done["cosr"], 2 * (i + 1))
                dve.wait_ge(done["kr_c"], i + 1)
                krope = kv_psum(i)[:, :, 1, :].rearrange("p g (s r) -> p g s r", s=2)
                dve.tensor_tensor(ru[:, part], krope,
                                  cosr[:, part].unsqueeze(2).broadcast_to([P, n, 2, HALF]), ALU.mult)
                after(dve.tensor_tensor(rw[:, part], krope,
                                        sinr[:, part].unsqueeze(2).broadcast_to([P, n, 2, HALF]),
                                        ALU.mult))
                dve.tensor_tensor(kr_[:, part, KVC:KVC + HALF], ru[:, part, 0, :], rw[:, part, 1, :],
                                  ALU.subtract).then_inc(done["kr_r"], 1)
                dve.tensor_tensor(kr_[:, part, KVC + HALF:], rw[:, part, 0, :], ru[:, part, 1, :],
                                  ALU.add).then_inc(done["kr_r"], 1)

            relative(0)
            rotate(0)
            dve.wait_ge(done["aq_ps"], 2)
            dve.tensor_copy(aq[0:QC, HP:, :],
                            bank[2][0:QC, :].rearrange("p (h c) -> p h c", c=KVC)).then_inc(
                done["aq_dve"], 1)
            relative(1)
            rotate(1)
            relative(2)
            rotate(2)
            dve.wait_ge(done["qt_ps"], 2)
            dve.tensor_copy(qt[:, :, HP:, :].rearrange("p c h q -> p h c q"),
                            bank[7][:].rearrange("p (h c q) -> p h c q", h=HP, q=QPC)).then_inc(
                done["qt_dve"], 1)
            dve.wait_ge(done["kt_ps"], 2)
            dve.tensor_copy(kt[:, 256:512], bank[4][:, 0:256]).then_inc(done["kt_dve"], 1)
            dve.wait_ge(done["maskb"], 1)
            first, second = slice(0, NCH // 2), slice(NCH // 2, NCH)
            for j, half in enumerate((first, second)):
                dve.wait_ge(done["s_ps"], j + 1)
                dve.scalar_tensor_tensor(
                    s[:, half, :], bank[1 + j][:, 0:4 * KPC].rearrange("p (c k) -> p c k", k=KPC),
                    QK_SCALE, maskb[:, half, :], ALU.mult, ALU.add).then_inc(done["s"], 1)
                dve.wait_ge(done["s"], j + 1)
                dve.tensor_reduce(nmax[:, half], s[:, half, :], AX.X, ALU.max,
                                  negate=True).then_inc(done["nmax"], 1)
            dve.wait_ge(done["nmax"], 2)
            dve.tensor_tensor(s[:, second, :], s[:, second, :], spread(nmax[:, second]),
                              ALU.add).then_inc(done["s_less_max"], 1)
            dve.wait_ge(done["exp"], NCH // 2)
            after(dve.reciprocal(rsum[:, first], psums[:, first]))
            dve.tensor_tensor(p[:, first, :], p[:, first, :], spread(rsum[:, first]),
                              ALU.mult).then_inc(done["p"], 1)
            dve.wait_ge(done["exp"], NCH // 2 + 1)
            after(dve.tensor_reduce(psums[:, second], p[:, second, :], AX.X, ALU.add))
            after(dve.reciprocal(rsum[:, second], psums[:, second]))
            dve.tensor_tensor(p[:, second, :], p[:, second, :], spread(rsum[:, second]),
                              ALU.mult).then_inc(done["p"], 1)
            dve.wait_ge(done["pt_ps"], 1)
            dve.tensor_copy(pt[0:KPC, 0:4, :].rearrange("k c n -> k (c n)"),
                            bank[3][0:KPC, :]).then_inc(done["pt_dve"], 1)
            for i in range(2):
                attended(dve.tensor_copy, dve, i).then_inc(done["ctx_dve"], 1)
            dve.wait_ge(landed["gla"], 16)
            a, b = place(GLA, "v")
            after(dve.tensor_reduce(wvsum[:], gla[:, :, a:b].rearrange("p c (h v) -> p c h v", v=DV),
                                    AX.X, ALU.add))
            for kc in range(DC):
                dve.scalar_tensor_tensor(wvc[:, kc], wvsum[:, kc].unsqueeze(2).broadcast_to([P, H, DV]),
                                         -1.0 / DV, gla_(kc, "v").rearrange("p (h v) -> p h v", v=DV),
                                         ALU.mult, ALU.add).then_inc(done["wvc"], 1)

            def residual(dst, psum, src, ready, signal):
                dve.wait_ge(ready, 1)
                dve.tensor_tensor(dst[:], psum[:, 0:P].rearrange("p (c t) -> p c t", c=DC), src[:],
                                  ALU.add).then_inc(signal, 1)

            def centre(dst, src, psum, ready, signal):
                dve.wait_ge(ready, 1)
                dve.tensor_tensor(dst[:], src[:],
                                  psum[:, 0:T].unsqueeze(1).broadcast_to([P, DC, T]),
                                  ALU.subtract).then_inc(signal, 1)

            dve.wait_ge(landed["xh"], 32)
            dve.wait_ge(done["y1_ps"], 1)
            dve.tensor_tensor(x1h[:], xh[:], bank[6][:, 0:P], ALU.add).then_inc(done["x1h"], 1)
            dve.wait_ge(done["x1t_ps"], 2)
            dve.tensor_copy(x1t[:, 1, :], bank[1][:, 0:T]).then_inc(done["x1t_dve"], 1)

            dve.wait_ge(done["x1t_act"], 1)
            dve.wait_ge(done["x1t_dve"], 1)
            centre(xm2t, x1t, bank[4], done["mean2_ps"], done["xm2t"])
            dve.wait_ge(done["kg1_ps"], 1)
            dve.tensor_copy(kg1[0:GLR, :], bank[1][0:GLR, 0:T]).then_inc(done["kg1"], 1)
            dve.wait_ge(done["rstd2"], 1)
            dve.wait_ge(done["kg_ps"], 1)
            dve.tensor_tensor(z[:], bank[7][:, 0:T], rstd2[:, 0:T], ALU.mult).then_inc(done["z"], 1)
            dve.wait_ge(done["v_ps"], 2)
            dve.wait_ge(done["rstd2"], 2)
            dve.tensor_scalar(vrep[:, 4:8], value_columns(3), rstd2[:, T:T + 1], None, ALU.mult).then_inc(done["v_dve"], 1)
            dve.wait_ge(done["z"], 1)
            dve.wait_ge(landed["kg2"], 16)
            dve.tensor_scalar(minz[:], z[:], kg2[:, P:P + 1], 0.0, ALU.add,
                              ALU.min).then_inc(done["minz"], 1)
            dve.wait_ge(done["qk_ps"], 1)
            dve.scalar_tensor_tensor(ks[:], bank[5][:, T:2 * T], GK_SCALE, rstd2[:, 0:T],
                                     ALU.mult, ALU.mult).then_inc(done["ks"], 1)
            dve.tensor_tensor(qs[:], bank[5][:, 0:T], rstd2[:, 0:T], ALU.mult).then_inc(
                done["qs"], 1)
            dve.wait_ge(done["minz"], 1)
            dve.wait_ge(done["lz"], 1)
            dve.tensor_tensor(logsig[:], minz[:], lz[:], ALU.subtract).then_inc(done["logsig"], 1)
            dve.wait_ge(done["ks"], 1)
            dve.wait_ge(done["qs"], 1)
            dve.wait_ge(done["gates_start"], 1)
            value_half = [slice(HALF_V * j, HALF_V * (j + 1)) for j in range(2)]

            def key_value(j):
                dve.wait_ge(done["vrep_ps"], 1)
                dve.tensor_tensor(kvt[:, value_half[j], :],
                                  bank[6 + j][:].rearrange("p (v t) -> p v t", t=T),
                                  ks[:].unsqueeze(1).broadcast_to([P, HALF_V, T]),
                                  ALU.mult).then_inc(done["kvt"], 1)

            def scan(j):
                dve.wait_ge(done["kvt"], j + 1)
                dve.wait_ge(done["gates"], j + 1)
                dve.tensor_tensor_scan(state[:, value_half[j], :].rearrange("p v t -> p (v t)"),
                                       gates[:, value_half[j], :].rearrange("p v t -> p (v t)"),
                                       kvt[:, value_half[j], :].rearrange("p v t -> p (v t)"),
                                       0.0, ALU.mult, ALU.add).then_inc(done["state"], 1)

            def query(i):
                a, b = Q_PIECES[i:i + 2]
                dve.wait_ge(done["state"], a // HALF_V + 1)
                dve.tensor_tensor(qstate[:, a:b, :], state[:, a:b, :],
                                  qs[:].unsqueeze(1).broadcast_to([P, b - a, T]),
                                  ALU.mult).then_inc(done["qstate"], 1)

            key_value(0)
            scan(0)
            key_value(1)
            query(0)
            scan(1)
            dve.wait_ge(landed["rows"], 16)
            dve.wait_ge(done["g_ps"], 1)
            dve.scalar_tensor_tensor(zg[0:T, :], bank[4][0:T, 0:D], rstd2[0:T, T:T + 1],
                                     rows_("bg"), ALU.mult, ALU.add).then_inc(done["zg"], 1)
            query(1)
            query(2)
            dve.wait_ge(done["osq"], 1)
            dve.tensor_reduce(ovar[0:T, :], osq[0:T], AX.X, ALU.add).then_inc(done["ovar"], 1)
            dve.wait_ge(done["sg"], 1)
            after(dve.tensor_tensor(ocs[0:T], bank[1][0:T, 0:D].rearrange("p (v h) -> p h v", h=H),
                                    sg[0:T, :].rearrange("p (h v) -> p h v", h=H), ALU.mult))
            dve.wait_ge(done["orstd"], 1)
            for hh in (slice(0, HP), slice(HP, H)):
                dve.tensor_tensor(og[0:T, hh], ocs[0:T, hh],
                                  orstd[0:T, hh].unsqueeze(2).broadcast_to([T, HP, DV]),
                                  ALU.mult).then_inc(done["og"], 1)
            dve.wait_ge(done["ogt_ps"], 2)
            dve.tensor_copy(ogt[:, T:], bank[0][:, 0:T]).then_inc(done["ogt_dve"], 1)
            residual(x2t, bank[3], x1t, done["y2_ps"], done["x2t"])

            dve.wait_ge(done["x2t"], 1)
            centre(xm3t, x2t, bank[2], done["mean3_ps"], done["xm3t"])
            dve.wait_ge(done["lg_ps"], 1)
            dve.wait_ge(done["rstd3"], 1)
            after(dve.scalar_tensor_tensor(logits[:], bank[5][:, 0:E], rstd3[:],
                                           rows_("router_b", P), ALU.mult, ALU.add))
            after(dve.max(top[:], logits[:]))
            dve.tensor_tensor(gap[:], top[:, 0:1], top[:, 1:2], ALU.subtract).then_inc(done["gap"], 1)
            dve.wait_ge(landed["expert_b"], 32)
            pieces = [(e, *piece) for e in range(EH) for piece in HPIECES[e]]

            def unsquashed(n):
                e, a, b, psum = pieces[n]
                dve.wait_ge(done["h_ps"], n + 1)
                dve.scalar_tensor_tensor(h[:, e, a:b], bank[psum][:, a:b], rstd3[:],
                                         expert_b[:, e * D + a:e * D + b], ALU.mult,
                                         ALU.add).then_inc(done["h"], 1)

            after(dve.max_index(topi[:], top[:], logits[:]))
            dve.tensor_copy(topf[:], topi[:]).then_inc(done["topf"], 1)
            unsquashed(0)
            unsquashed(1)
            dve.wait_ge(done["tgap"], 1)
            dve.wait_ge(done["hotpm"], 2)
            for j, half in enumerate(halves):
                ex = slice(j * EH, (j + 1) * EH)
                dve.scalar_tensor_tensor(fw[half, :], hdiff[half, ex], tgap[half, :], hsum[half, ex],
                                         ALU.mult, ALU.add).then_inc(done["fw"], 1)

            def combine(n):
                e, a, b, _ = pieces[n]
                dve.wait_ge(done["hs"], n + 1)
                dve.wait_ge(done["fw"], 2)
                if e == 0:
                    ins = dve.tensor_scalar(comb[:, 0, :], hs[:, 0, :], fw[:, 0:1], None, ALU.mult)
                else:
                    dve.wait_ge(done["comb"], e)
                    ins = dve.scalar_tensor_tensor(comb[:, e, a:b], hs[:, e, a:b], fw[:, e:e + 1],
                                                   comb[:, e - 1, a:b], ALU.mult, ALU.add)
                ins.then_inc(done["comb"], 1)

            combine(0)
            unsquashed(2)
            combine(1)
            unsquashed(3)
            unsquashed(4)
            for n in range(2, len(pieces)):
                combine(n)
            for kc in range(DC):
                dve.wait_ge(done["combt_ps"], kc + 1)
                dve.tensor_copy(combt[:, kc * T:(kc + 1) * T],
                                bank[(5, 0)[kc]][:, 0:T]).then_inc(done["combt"], 1)
            dve.wait_ge(done["xb"], 1)
            dve.wait_ge(done["y3_ps"], 1)
            dve.tensor_tensor(y[0:T, :], xb[0:T, :], bank[3][0:T, 0:D], ALU.add).then_inc(done["y"], 1)
            dve.wait_ge(done["y"], 1)
            after(dve.tensor_tensor(yn[0:T, :], y[0:T, :], rows_("norm_w"), ALU.mult))
            dve.wait_ge(done["yr"], 1)
            dve.scalar_tensor_tensor(fin[0:T, :], yn[0:T, :], yr[0:T, :], x2[0:T, :],
                                     ALU.mult, ALU.add).then_inc(done["fin"], 1)


def pack(parts, values, rows_=P):
    out = np.zeros((rows_, width(parts)), np.float32)
    for name in parts:
        if name in values:
            a, b = place(parts, name)
            v = values[name]
            out[:v.shape[0], a:a + v.shape[1]] = v
    return out


def by_chunk(w):
    return np.ascontiguousarray(w.reshape(DC, P, -1).transpose(1, 0, 2)).reshape(P, -1)


def rope_tables():
    freq = (1.0 / np.float32(10000.0) ** (np.arange(HALF, dtype=np.float32) / np.float32(HALF))).astype(np.float32)
    ang = (np.arange(LK, dtype=np.float32)[:, None] * freq).astype(np.float32)
    return np.cos(ang).astype(np.float32), np.sin(ang).astype(np.float32)


def kernel(**inputs):
    import concourse.bacc as bacc
    from concourse.bass_utils import run_bass_kernel_spmd

    a = {k: np.asarray(v) for k, v in inputs.items()}
    w = {k[3:]: v for k, v in a.items() if k.startswith("L0_")}
    cos, sin = rope_tables()

    key = np.arange(NG * P) % NKEY
    query = (key // WIN).reshape(NG, P).T
    seg = a["itok_BxS_0_1023"].reshape(T)
    seg_in = np.concatenate([seg[query], np.tile(seg, (P, 1)),
                             ((key % WIN) - LOOKBACK).reshape(NG, P).T,
                             np.tile(np.arange(WIN) + int(SHIFT), (P, 1))], axis=1).astype(seg.dtype)

    c1 = pack(C1, dict(ident=np.eye(P, dtype=np.float32), dq=by_chunk(w["xattn_W_dq"])))
    own = np.arange(P)[:, None] % QPC == np.arange(KPC)[None, :] // WIN
    c2 = pack(C2, dict(
        kvct=w["xattn_W_kvc"].reshape(DC, P, KVC).transpose(0, 2, 1).reshape(P, P),
        kr=np.tile(w["xattn_W_kr"], (DC, 1)), kvc=by_chunk(w["xattn_W_kvc"]),
        block=np.where(own, 0.0, NEG),
        cosq=cos[query].reshape(P, -1), sinq=sin[query].reshape(P, -1),
        headsum=(np.arange(P)[:, None] // DK == np.arange(H)[None, :]),
        twice=np.tile(np.eye(T), (2, 1)), iota=np.tile(np.arange(E), (P, 1))))

    def heads(m, first):
        return m.reshape(first, H, -1)

    uqk = np.concatenate([heads(w["xattn_W_uq"], QC).transpose(2, 1, 0),
                          heads(w["xattn_W_uk"], KVC).transpose(2, 1, 0)], axis=2).reshape(P, -1)
    g = np.concatenate([w[f"attn_{n}"].T.reshape(DC, P, -1)
                        for n in ("Wq", "Wk", "Wkg1", "Wv", "Wg", "Wo")], axis=2)
    kg2 = np.zeros((P, P + 1), np.float32)
    kg2[:GLR, :P] = w["attn_Wkg2"].T
    kg2[:, P] = w["attn_bkg2"]
    arrays = dict(
        seg=seg_in,
        x=a["x"].reshape(T, D),
        c1=c1, c2=c2,
        ctx=np.concatenate([a["ctx_2048"].reshape(LK, D), cos, sin], axis=1),
        uqk=uqk,
        qr=w["xattn_W_qr"],
        uv=heads(w["xattn_W_uv"], KVC).transpose(2, 1, 0).reshape(P, -1),
        wo=w["xattn_W_o"].reshape(H, HD, D).transpose(1, 0, 2).reshape(P, -1),
        gla=g.transpose(1, 0, 2).reshape(P, -1),
        kg2=kg2,
        rows=np.concatenate([w["attn_bg"], w["ffn_proj_b"], w["ffn_norm_w"], w["ffn_router_b"]])[None],
        router=by_chunk(w["ffn_router_w"]),
        expert=w["ffn_expert_w"].reshape(E, DC, P, D).transpose(2, 1, 0, 3).reshape(P, -1),
        expert_b=w["ffn_expert_b"].reshape(2, EH * D),
        proj=by_chunk(w["ffn_proj_w"]))
    arrays = {f"in_{k}": np.ascontiguousarray(v) for k, v in arrays.items()}

    nc = bacc.Bacc("TRN2", target_bir_lowering=False, num_devices=1)
    args = [nc.dram_tensor(k, v.shape, mybir.dt.from_np(v.dtype), kind="ExternalInput").ap()
            for k, v in arrays.items()]
    out = nc.dram_tensor("out", (T, D), F32, kind="ExternalOutput").ap()
    block_kernel(nc, *args, out)
    r = run_bass_kernel_spmd(nc, [arrays], core_ids=[0])
    return r.results[0]["out"].reshape(1, T, D)
```
